# Optimizing a Trainium2 kernel written in Bass

```python
import numpy as np
import jax
import jax.numpy as jnp

def _softmax(x, axis=-1):
    return jax.nn.softmax(x, axis=axis)

def _gelu(x):
    return jax.nn.gelu(x, approximate=True)

def _silu(x):
    return jax.nn.silu(x)

def _sigmoid(x):
    return jax.nn.sigmoid(x)

def _layernorm(x, axis=-1, eps=1e-05):
    m = jnp.mean(x, axis=axis, keepdims=True)
    v = jnp.var(x, axis=axis, keepdims=True)
    return (x - m) / jnp.sqrt(v + eps)

def _scatter_add(tgt, idx, src, axis=0):
    return tgt.at[idx].add(src)

def _segment_sum(src, seg, n):
    return jax.ops.segment_sum(src, seg, n)
kernel_name = 'mk_gnn_ffn_d1_gnn_r32_004378'

def setup_inputs(seed: int=0):
    np.random.seed(seed)
    _w = jnp.asarray

    def _rec_inputs():
        import jax
        import jax.numpy as jnp
        _gk = jax.random.key(seed)
        x = -0.0002117 + 1 * jax.random.normal(jax.random.fold_in(_gk, 1), (3125, 256), jnp.float32)
        src = jax.random.randint(jax.random.fold_in(_gk, 2), (50000,), 0, 3125, jnp.int32)
        dst = jnp.minimum((3125 * jax.random.uniform(jax.random.fold_in(_gk, 3), (50000,)) ** 2.0).astype(jnp.int32), 99999)
        _o = jnp.argsort(dst, stable=True)
        src = src[_o]
        dst = dst[_o]
        edge_weight = jax.random.uniform(jax.random.fold_in(_gk, 12), (50000,), jnp.float32, 0.0, 1)
        return (x, src, dst, edge_weight)
    x, src, dst, edge_weight = _rec_inputs()

    def _L0_gnn_setup():
        import jax, jax.numpy as jnp
        import numpy as np
        N = 3125
        E = 50000
        D_IN = 256
        D_OUT = 256
        NEG_SLOPE = 0.01
        key = jax.random.key(seed)
        k1, k2, k3, k4, k5, k6 = jax.random.split(key, 6)
        ego_embeddings = jax.random.normal(k1, (N, D_IN), dtype=jnp.float32)
        rows = jax.random.randint(k2, (E,), 0, N, dtype=jnp.int32)
        cols = jax.random.randint(k3, (E,), 0, N, dtype=jnp.int32)
        vals = jax.random.uniform(k4, (E,), dtype=jnp.float32)
        W1 = jax.random.normal(k5, (D_IN, D_OUT), dtype=jnp.float32) * (1.0 / np.sqrt(D_IN))
        W2 = jax.random.normal(k6, (D_IN, D_OUT), dtype=jnp.float32) * (1.0 / np.sqrt(D_IN))
        b1 = jnp.zeros((D_OUT,), dtype=jnp.float32)
        b2 = jnp.zeros((D_OUT,), dtype=jnp.float32)
        return {'ego_embeddings': ego_embeddings, 'vals': vals, 'W1': W1, 'b1': b1, 'W2': W2, 'b2': b2, 'rows': rows, 'cols': cols}
    _L0_gnn_all = _L0_gnn_setup()
    _L0_gnn_in = {k: v for k, v in _L0_gnn_all.items() if k in ('W1', 'b1', 'W2', 'b2')}
    del _L0_gnn_all

    def _L0_ffn_setup():
        import jax, jax.numpy as jnp
        import numpy as np
        B, S, H, F, E, K = (8, 128, 256, 512, 16, 2)
        EPS = 1e-05
        key = jax.random.key(seed)
        ks = jax.random.split(key, 9)
        sc = 0.02
        return {'x': jax.random.normal(ks[0], (B, S, H), dtype=jnp.float32), 'gate_w': jax.random.normal(ks[1], (H, E), dtype=jnp.float32) * sc, 'gate_b': jnp.zeros((E,), dtype=jnp.float32), 'w1': jax.random.normal(ks[2], (E, H, F), dtype=jnp.float32) * sc, 'b1': jnp.zeros((E, F), dtype=jnp.float32), 'w2': jax.random.normal(ks[3], (E, F, H), dtype=jnp.float32) * sc, 'b2': jnp.zeros((E, H), dtype=jnp.float32), 'gamma': jnp.ones((H,), dtype=jnp.float32), 'beta': jnp.zeros((H,), dtype=jnp.float32)}
    _L0_ffn_all = _L0_ffn_setup()
    _L0_ffn_in = {k: v for k, v in _L0_ffn_all.items() if k in ('gate_w', 'gate_b', 'w1', 'b1', 'w2', 'b2', 'gamma', 'beta')}
    del _L0_ffn_all
    return {'x': x, 'src': src, 'dst': dst, 'edge_weight': edge_weight, 'L0_gnn_W1': _L0_gnn_in['W1'], 'L0_gnn_b1': _L0_gnn_in['b1'], 'L0_gnn_W2': _L0_gnn_in['W2'], 'L0_gnn_b2': _L0_gnn_in['b2'], 'L0_ffn_gate_w': _L0_ffn_in['gate_w'], 'L0_ffn_gate_b': _L0_ffn_in['gate_b'], 'L0_ffn_w1': _L0_ffn_in['w1'], 'L0_ffn_b1': _L0_ffn_in['b1'], 'L0_ffn_w2': _L0_ffn_in['w2'], 'L0_ffn_b2': _L0_ffn_in['b2'], 'L0_ffn_gamma': _L0_ffn_in['gamma'], 'L0_ffn_beta': _L0_ffn_in['beta']}

def reference(x, src, dst, edge_weight, L0_gnn_W1, L0_gnn_b1, L0_gnn_W2, L0_gnn_b2, L0_ffn_gate_w, L0_ffn_gate_b, L0_ffn_w1, L0_ffn_b1, L0_ffn_w2, L0_ffn_b2, L0_ffn_gamma, L0_ffn_beta):
    import jax
    import jax.numpy as jnp

    def _L0_gnn_ref(ego_embeddings, vals, W1, b1, W2, b2, rows, cols):
        import jax, jax.numpy as jnp
        import numpy as np
        N = 3125
        E = 50000
        D_IN = 256
        D_OUT = 256
        NEG_SLOPE = 0.01
        msgs = vals[:, None] * ego_embeddings[cols]
        side = jax.ops.segment_sum(msgs, rows, num_segments=N)
        sum_emb = jax.nn.leaky_relu((ego_embeddings + side) @ W1 + b1, NEG_SLOPE)
        bi_emb = jax.nn.leaky_relu(ego_embeddings * side @ W2 + b2, NEG_SLOPE)
        return sum_emb + bi_emb

    def _L0_ffn_ref(x, gate_w, gate_b, w1, b1, w2, b2, gamma, beta):
        import jax, jax.numpy as jnp
        import numpy as np
        B, S, H, F, E, K = (8, 128, 256, 512, 16, 2)
        EPS = 1e-05
        gate_logits = x @ gate_w + gate_b
        topk_vals, topk_idx = jax.lax.top_k(gate_logits, K)
        topk_w = jax.nn.softmax(topk_vals, axis=-1)
        h = jax.nn.relu(jnp.einsum('bsh,ehf->bsef', x, w1) + b1)
        expert_out = jnp.einsum('bsef,efh->bseh', h, w2) + b2
        sel = jnp.take_along_axis(expert_out, topk_idx[:, :, :, None], axis=2)
        moe = jnp.sum(topk_w[..., None] * sel, axis=2)
        y = x + moe
        mu = jnp.mean(y, axis=-1, keepdims=True)
        var = jnp.var(y, axis=-1, keepdims=True)
        return (y - mu) / jnp.sqrt(var + EPS) * gamma + beta
    x = x + _L0_gnn_ref(_layernorm(x, axis=-1), edge_weight, L0_gnn_W1, L0_gnn_b1, L0_gnn_W2, L0_gnn_b2, src, dst)
    x = x + _L0_ffn_ref(_layernorm(x, axis=-1)[None], L0_ffn_gate_w, L0_ffn_gate_b, L0_ffn_w1, L0_ffn_b1, L0_ffn_w2, L0_ffn_b2, L0_ffn_gamma, L0_ffn_beta)[0]
    return x

_drawn_inputs = setup_inputs


def setup_inputs(seed=0):
    import zlib

    import numpy as np

    out = dict(_drawn_inputs(seed))
    spreads = {'L0_gnn_b1': (0.0, 0.284),
     'L0_gnn_b2': (0.0, 0.274),
     'L0_ffn_gate_b': (0.0, 0.431),
     'L0_ffn_b1': (0.0, 0.8),
     'L0_ffn_b2': (0.0, 0.412),
     'L0_ffn_gamma': (1.0, 0.2),
     'L0_ffn_beta': (0.0, 0.306)}
    factors = {'L0_ffn_w1': 3.457, 'L0_ffn_w2': 2.764}
    for name, (base, spread) in spreads.items():
        noise = np.random.default_rng([zlib.crc32(name.encode()), seed]).standard_normal(out[name].shape)
        drawn = base * np.exp(spread * noise) if base else spread * noise
        out[name] = jnp.asarray(drawn.astype(out[name].dtype))
    for name, factor in factors.items():
        out[name] = (out[name] * factor).astype(out[name].dtype)
    return out
```

```python
import concourse.bass as bass
from concourse import mybir
from contextlib import ExitStack

f32 = mybir.dt.float32
bf16 = mybir.dt.bfloat16
f16 = mybir.dt.float16
i32 = mybir.dt.int32
ALU = mybir.AluOpType
ACT = mybir.ActivationFunctionType
AX = mybir.AxisListType
DVE = mybir.EngineType.DVE
SP = mybir.EngineType.SP
ACTE = mybir.EngineType.Activation

P = 128
SH = 7
N, D = 3125, 256
KD = D // P
E = 50000
NT = -(-N // P)
LAST = N - (NT - 1) * P
UE = 8
EC = -(-E // P // UE) * UE
ELAST = E - (P - 1) * EC
NG = (EC * P + NT * (P - 1)) // P
DOFF = N // 2
RING = 16
MR = 8
PR = 4
X, F, K = 16, 512, 2
KF = F // P
BS = 256
NB = (K * N + X * (BS - 1)) // BS
NS = NB * (BS // P)
NA = -(-K * NT // UE) * UE
NOROW = 8192
BIG = 3.0e38
YR = 8
EPS = 1e-5
SLOPE = 0.01

assert NG % RING == 0 and NT % 2 == 1 and NB % 2 == 0 and (EC // UE) % 2 == 1 and 0 < ELAST <= EC
assert (NT - 1) % YR == 0 and K * NT < NA and 2 * (DOFF + 1) < NOROW


def build(nc, x, src, dst, edge_weight, gW1, gb1, gW2, gb2, gate_w, gate_b, w1, b1, w2, b2, gamma, beta, out):
    h_dram = nc.dram_tensor("h_dram", (NT * P, D), f32).ap()
    z_dram = nc.dram_tensor("z_dram", (NT * P, D), f32).ap()
    y_dram = nc.dram_tensor("y_dram", (NT * P * K, D), f32).ap()

    with ExitStack() as ctx:
        def sb(name, shape, dt=f32):
            return ctx.enter_context(nc.sbuf_tensor(name, shape, dt))

        def sem(name):
            return ctx.enter_context(nc.semaphore(name))

        bank = [ctx.enter_context(nc.psum_tensor(f"bank{i}", [P, 512], f32)) for i in range(8)]

        slots16 = sb("slots16", [P, P, UE], f16)
        slots32 = sb("slots32", [P, P])
        groups16 = sb("groups16", [P, NG], f16)
        below = sb("below", [P, P])
        ones = sb("ones", [P, P])
        ident = sb("ident", [P, P])
        zeros16 = sb("zeros16", [P, NG], bf16)
        eps_col = sb("eps_col", [P, 1])
        tokens = sb("tokens", [P, NT])
        valid = sb("valid", [P, 1])
        experts = sb("experts", [P, X, NT])

        xs = sb("xs", [P, NT, D])
        hs = sb("hs", [P, NT, D])
        stats = sb("stats", [P, NT, 6])
        mv = sb("mv", [P, NT, 2])
        ln = [sb(f"ln{i}", [P, NT]) for i in range(4)]

        src_i = sb("src_i", [P, EC], i32)
        dst_i = sb("dst_i", [P, EC], i32)
        ew = sb("ew", [P, EC])
        bin_f = sb("bin_f", [P, EC])
        tmp_i = sb("tmp_i", [P, EC], i32)
        tmp2_i = sb("tmp2_i", [P, EC], i32)
        pos_f = sb("pos_f", [P, EC])
        group_f = sb("group_f", [P, EC])
        slot16 = sb("slot16", [P, EC], f16)
        val16 = [sb(f"val16_{i}", [P, EC], f16 if i < 2 else bf16) for i in range(5)]
        inbin = sb("inbin", [P, NT * EC], bf16)
        scan = sb("scan", [P, NT * EC])
        inbin_v = inbin[:, :].rearrange("p (b c) -> p b c", c=EC)
        scan_v = scan[:, :].rearrange("p (b c) -> p b c", c=EC)
        ones_e = sb("ones_e", [P, EC], bf16)
        cnt = sb("cnt", [P, NT])
        base = sb("base", [P, NT])
        tot_i = sb("tot_i", [P, NT], i32)
        gend = sb("gend", [P, NT])
        gfirst = sb("gfirst", [P, NT])
        first_col = sb("first_col", [P, 1])
        reached = sb("reached", [P, NG], bf16)
        bin_i = sb("bin_i", [P, NG], i32)
        at_slot = sb("at_slot", [P, 2, P, UE], bf16)
        put = sb("put", [P, 2, 5, P * UE], bf16)
        put_v = put[:, :, :, :].rearrange("p r f (s u) -> p r f s u", u=UE)
        in_group = sb("in_group", [P, 2, UE, NG], bf16)

        node_i = sb("node_i", [P, NG], i32)
        slot_src = sb("slot_src", [P, NG])
        slot_ew = sb("slot_ew", [P, NG])
        stage = sb("stage", [P, 2, 8], i32)
        side = scan[:, 0:NT * D].rearrange("p (t d) -> p t d", d=D)
        free0 = NT * D
        uv = scan[:, free0:free0 + 4 * D].rearrange("p (r k d) -> p r k d", r=2, k=2)
        uvT = scan[:, free0 + 4 * D:free0 + 8 * D].rearrange("p (r c n) -> p r c n", r=2, c=4)
        lk = scan[:, free0 + 8 * D:free0 + 12 * D].rearrange("p (r k d) -> p r k d", r=2, k=2)
        ring = put[:, :, :, :].rearrange("p a b c -> p (a b c)")[:, 0:2 * RING * D].bitcast(f32).rearrange("p (r d) -> p r d", d=D)
        gw = sb("gw", [P, 2, KD, D])
        gb = sb("gb", [1, 2, D])
        gatew = sb("gatew", [P, KD, X])
        gateb = sb("gateb", [P, X])

        YB = ((5, 6), (7, 0))
        at = [0]

        def part(*shape):
            n = 1
            for k in shape:
                n *= k
            at[0] += n
            assert at[0] <= NT * EC
            names = " ".join("abcd"[:len(shape)])
            view = scan[:, at[0] - n:at[0]]
            return view.rearrange(f"p ({names}) -> p {names}", **dict(zip("abcd", shape))) if len(shape) > 1 else view

        logits = part(X, NT)
        is_top = part(X, NT)
        chosen = [part(X, NT) for _ in range(K)]
        rank = part(X, NT)
        spread = part(X, NT)
        zTg = part(2, KD, P)
        y_sb = part(2, 2, D)
        y_in = part(YR, K, D)
        top = [sb(f"top{k}", [P, NT]) for k in range(K)]
        pick = sb("pick", [P, NT])
        gain = [sb(f"gain{k}", [P, NT]) for k in range(K)]
        bases = sb("bases", [P, X])
        btot_i = sb("btot_i", [P, X], i32)
        bfirst = sb("bfirst", [P, X])
        bend = sb("bend", [P, X])
        place_f = sb("place_f", [P, NA])
        place_i = sb("place_i", [P, NA], i32)
        place2_i = sb("place2_i", [P, NA], i32)
        pgroup_f = sb("pgroup_f", [P, NA])
        pslot16 = sb("pslot16", [P, NA], f16)
        ptok16 = sb("ptok16", [P, NA], f16)
        pk16 = sb("pk16", [P, NA], f16)
        breached = sb("breached", [P, NB], bf16)
        expert_i = sb("expert_i", [P, NB], i32)
        row_f = sb("row_f", [P, NS])
        empty_f = sb("empty_f", [P, NS])
        row_i = sb("row_i", [P, NS], i32)
        token_i = sb("token_i", [P, NS], i32)
        tstage = sb("tstage", [P, 2, 2], i32)
        rstage = sb("rstage", [P, 2, 2], i32)
        wring = inbin[:, 0:2 * 2 * 2 * KD * F].bitcast(f32).rearrange("p (r w n) -> p r w n", r=2, w=2)
        w1_sb = wring[:, :, 0, :].rearrange("p r (c f) -> p r c f", c=KD)
        w2_sb = wring[:, :, 1, :].rearrange("p r (c d) -> p r c d", c=KF)
        b2_sb = sb("b2_sb", [1, 2, D])
        b1_rows = sb("b1_rows", [X * KF, P])
        b1T = sb("b1T", [P, X * KF])
        gam = sb("gam", [P, D])
        bet = sb("bet", [P, D])
        y_last = sb("y_last", [P, K, D])
        work = put[:, :, :, :].rearrange("p a b c -> p (a b c)").bitcast(f32)
        zg = work[:, 0:4 * D].rearrange("p (r s d) -> p r s d", r=2, s=2)
        zT = work[:, 4 * D:8 * D].rearrange("p (r c n) -> p r c n", r=2, c=KD)
        hT = work[:, 8 * D:16 * D].rearrange("p (r c n) -> p r c n", r=2, c=KF)

        mat = in_group[:, :, :, :].rearrange("p a b c -> p (a b c)")[:, 0:2 * MR * P].bitcast(f32).rearrange("p (r s) -> p r s", s=P)

        s_const = sem("s_const")
        s_pad = sem("s_pad")
        s_edge = sem("s_edge")
        s_x = sem("s_x")
        s_wload = sem("s_wload")
        s_v = sem("s_v")
        s_cnt = sem("s_cnt")
        s_off = sem("s_off")
        s_var = sem("s_var")
        s_std = sem("s_std")
        s_rstd = sem("s_rstd")
        s_h = sem("s_h")
        s_htable = sem("s_htable")
        s_first = sem("s_first")
        s_firstT = sem("s_firstT")
        s_reached = sem("s_reached")
        s_binrow = sem("s_binrow")
        s_at = sem("s_at")
        s_onehot = sem("s_onehot")
        s_onehot_free = sem("s_onehot_free")
        s_sorted = sem("s_sorted")
        s_lists = sem("s_lists")
        s_stage = sem("s_stage")
        s_turn = sem("s_turn")
        s_got = [sem(f"s_got{i}") for i in range(RING)]
        s_mat = sem("s_mat")
        s_part = sem("s_part")
        s_acc = sem("s_acc")
        s_uv = sem("s_uv")
        s_uvT = sem("s_uvT")
        s_uvTc = sem("s_uvTc")
        s_o = sem("s_o")
        s_lk = sem("s_lk")
        s_slope = sem("s_slope")
        s_x1 = sem("s_x1")
        s_z = sem("s_z")
        s_ztable = sem("s_ztable")
        s_zTg = sem("s_zTg")
        s_zTgc = sem("s_zTgc")
        s_logit = sem("s_logit")
        s_gap = sem("s_gap")
        s_exp = sem("s_exp")
        s_bcnt = sem("s_bcnt")
        s_boff = sem("s_boff")
        s_bfirst = sem("s_bfirst")
        s_bfirstT = sem("s_bfirstT")
        s_breached = sem("s_breached")
        s_brow = sem("s_brow")
        s_blocks = sem("s_blocks")
        s_b1T = sem("s_b1T")
        s_b1 = sem("s_b1")
        s_pat = sem("s_pat")
        s_pone = sem("s_pone")
        s_pfree = sem("s_pfree")
        s_placed = sem("s_placed")
        s_routes = sem("s_routes")
        s_tstage = sem("s_tstage")
        s_rstage = sem("s_rstage")
        s_zg = [sem(f"s_zg{i}") for i in range(4)]
        s_w = [sem(f"s_w{i}") for i in range(2)]
        s_zgT = sem("s_zgT")
        s_zTc = sem("s_zTc")
        s_hid = sem("s_hid")
        s_relu = sem("s_relu")
        s_y = sem("s_y")
        s_ysb = sem("s_ysb")
        s_yout = [sem(f"s_yout{i}") for i in range(2)]
        s_yin = [sem(f"s_yin{i}") for i in range(YR)]
        s_ylast = sem("s_ylast")
        s_sum = sem("s_sum")
        s_norm = sem("s_norm")
        s_fin = sem("s_fin")
        s_out = sem("s_out")

        nodes_v = slice(0, (NT - 1) * P)

        def tiled(dram):
            return dram[nodes_v, :].rearrange("(t p) d -> p t d", p=P)

        block = ctx.enter_context(nc.Block())

        @block.sync
        def _(sp):
            sp.wait_ge(s_pad, 4)
            for tile, dram in ((src_i, src), (dst_i, dst), (ew, edge_weight)):
                sp.dma_start(tile[0:P - 1, :], dram[0:(P - 1) * EC].rearrange("(p c) -> p c", c=EC)).then_inc(s_edge, 16)
                sp.dma_start(tile[P - 1:P, 0:ELAST], dram[(P - 1) * EC:E].rearrange("(p c) -> p c", p=1)).then_inc(s_edge, 16)
            sp.dma_start(xs[:, 0:NT - 1, :], tiled(x)).then_inc(s_x, 16)
            sp.dma_start(xs[0:LAST, NT - 1, :], x[(NT - 1) * P:N, :]).then_inc(s_x, 16)
            for k, (w, b) in enumerate(((gW1, gb1), (gW2, gb2))):
                sp.dma_start(gw[:, k, :, :], w.rearrange("(c p) n -> p c n", p=P)).then_inc(s_wload, 16)
                sp.dma_start(gb[:, k, :], b.rearrange("(a n) -> a n", a=1)).then_inc(s_wload, 16)
            sp.dma_start(gatew[:, :, :], gate_w.rearrange("(c p) n -> p c n", p=P)).then_inc(s_wload, 16)
            for tile, dram in ((gateb, gate_b), (gam, gamma), (bet, beta)):
                sp.dma_start(tile[:, :], dram.rearrange("(a n) -> a n", a=1).broadcast_to(tile.shape)).then_inc(s_wload, 16)
            sp.dma_start(b1_rows[:, :], b1.rearrange("x (c p) -> (x c) p", p=P)).then_inc(s_wload, 16)
            sp.wait_ge(s_h, NT)
            sp.dma_start(h_dram.rearrange("(t p) d -> p t d", p=P), hs[:, :, :]).then_inc(s_htable, 16)
            sp.wait_ge(s_z, NT)
            sp.dma_start(z_dram.rearrange("(t p) d -> p t d", p=P), hs[:, :, :]).then_inc(s_ztable, 16)

            sp.wait_ge(s_blocks, 1)
            with sp.Fori(0, NB // 2) as i:
                _, es = nc.values_load_multi_w_load_instructions(expert_i[0:1, bass.ds(i * 2, 2)], engines=[SP], min_val=0, max_val=X - 1)
                for r in range(2):
                    e = bass.ds(es[r], 1)
                    sp.wait_ge(s_y, i * 2 + (r + 1))
                    sp.dma_start(w1_sb[:, r, :, :], w1[e, :, :].rearrange("x (c p) f -> p (x c) f", p=P)).then_inc(s_w[r], 16)
                    sp.dma_start(w2_sb[:, r, :, :], w2[e, :, :].rearrange("x (c p) d -> p (x c) d", p=P)).then_inc(s_w[r], 16)
                    sp.dma_start(b2_sb[:, r, :], b2[e, :]).then_inc(s_w[r], 16)

            for r in range(2):
                sp.wait_ge(s_yout[r], NB // 2 * 32)
            y_rows = y_dram.rearrange("(t p k) d -> t p k d", p=P, k=K)
            sp.dma_start(y_last[0:LAST, :, :], y_rows[NT - 1, 0:LAST, :, :]).then_inc(s_ylast, 16)
            with sp.Fori(0, (NT - 1) // YR) as i:
                for j in range(YR):
                    sp.wait_ge(s_sum, (i * YR + j + 1) * 3)
                    sp.dma_start(y_in[:, j, :, :], y_rows[bass.ds(i * YR + j, 1), :, :, :].rearrange("t p k d -> (t p) k d")).then_inc(s_yin[j], 16)

            with sp.Fori(0, NT - 1) as t:
                sp.wait_ge(s_fin, t * 2 + 2)
                sp.dma_start(out[bass.ds(t * P, P), :], hs[:, bass.ds(t, 1), :].rearrange("p t d -> p (t d)")).then_inc(s_out, 16)
            sp.wait_ge(s_fin, NT * 2)
            sp.dma_start(out[(NT - 1) * P:N, :], hs[0:LAST, NT - 1, :]).then_inc(s_out, 16)
            sp.wait_ge(s_out, NT * 16)

        @block.gpsimd
        def _(gp):
            made = [0]

            def const(ins):
                made[0] += 1
                ins.then_inc(s_const, 1)
                gp.wait_ge(s_const, made[0])

            const(gp.iota(slots16[:, :, :], pattern=[[1, P], [0, UE]], base=0, channel_multiplier=0, allow_small_or_imprecise_dtypes=True))
            const(gp.iota(slots32[:, :], pattern=[[1, P]], base=0, channel_multiplier=0, allow_small_or_imprecise_dtypes=True))
            const(gp.iota(groups16[:, :], pattern=[[1, NG]], base=0, channel_multiplier=0, allow_small_or_imprecise_dtypes=True))
            const(gp.memset(ones[:, :], 1.0))
            const(gp.memset(ones_e[:, :], 1.0))
            const(gp.memset(zeros16[:, :], 0.0))
            const(gp.memset(eps_col[:, :], EPS))
            const(gp.affine_select(out=below[:, :], in_=ones[:, :], compare_op=ALU.is_gt, fill=0.0, base=0,
                                   pattern=[[1, P]], channel_multiplier=-1))
            const(gp.affine_select(out=ident[:, :], in_=ones[:, :], compare_op=ALU.is_equal, fill=0.0, base=0,
                                   pattern=[[1, P]], channel_multiplier=-1))
            const(gp.affine_select(out=valid[:, :], in_=ones[:, 0:1], compare_op=ALU.is_gt, fill=0.0, base=LAST,
                                   pattern=[[0, 1]], channel_multiplier=-1))
            const(gp.iota(experts[:, :, :], pattern=[[1, X], [0, NT]], base=-X, channel_multiplier=0, allow_small_or_imprecise_dtypes=True))

            const(gp.iota(tokens[:, :], pattern=[[P, NT]], base=-DOFF, channel_multiplier=1, allow_small_or_imprecise_dtypes=True))

            gp.wait_ge(s_lists, 1)
            gp.wait_ge(s_htable, 16)
            gp.wait_ge(s_sorted, 1)
            with gp.Fori(0, NG // RING) as i:
                for half in range(2):
                    gp.wait_ge(s_part, i * RING + (half * 8 + 8))
                    gp.tensor_copy(stage[:, half, :], node_i[:, bass.ds(i * RING + half * 8, 8)]).then_inc(s_stage, 1)
                    gp.wait_ge(s_stage, i * 2 + (half + 1))
                    gp.sem_inc(s_turn, 1)
                    for j in range(8):
                        slot = half * 8 + j
                        gp.indirect_dma_start(ring[:, slot, :], None, h_dram,
                                              bass.IndirectOffsetOnAxis(stage[:, half, j:j + 1], 0)).then_inc(s_got[slot], 16)

            gp.wait_ge(s_acc, NG + PR)
            def uv_tile(t, r):
                gp.wait_ge(s_uvT, t + 1)
                gp.tensor_tensor(uv[:, r, 0, :], hs[:, t, :], side[:, t, :], ALU.add)
                gp.tensor_tensor(uv[:, r, 1, :], hs[:, t, :], side[:, t, :], ALU.mult).then_inc(s_uv, 1)

            with gp.Fori(0, NT // 2) as i:
                for r in range(2):
                    uv_tile(i * 2 + r, r)
            uv_tile(NT - 1, 0)

            gp.wait_ge(s_routes, 2)
            gp.wait_ge(s_ztable, 16)

            def gather(b, r):
                gp.wait_ge(s_zgT, b + 1)
                gp.tensor_copy(tstage[:, r, :], token_i[:, bass.ds(b * 2, 2)]).then_inc(s_tstage, 1)
                gp.wait_ge(s_tstage, b + 1)
                gp.sem_inc(s_turn, 1)
                for q in range(2):
                    gp.indirect_dma_start(zg[:, r, q, :], None, z_dram, bass.IndirectOffsetOnAxis(tstage[:, r, q:q + 1], 0)).then_inc(s_zg[r * 2 + q], 16)

            def scatter(b, r):
                gp.wait_ge(s_ysb, b * 2 + 6)
                gp.tensor_copy(rstage[:, r, :], row_i[:, bass.ds(b * 2, 2)]).then_inc(s_rstage, 1)
                gp.wait_ge(s_rstage, b + 1)
                gp.sem_inc(s_turn, 1)
                for q in range(2):
                    gp.indirect_dma_start(y_dram, bass.IndirectOffsetOnAxis(rstage[:, r, q:q + 1], 0), y_sb[:, r, q, :], None,
                                          bounds_check=K * N - 1, oob_is_err=False).then_inc(s_yout[r], 16)

            for r in range(2):
                gather(r, r)
            with gp.Fori(0, NB // 2 - 1) as i:
                for r in range(2):
                    gather(i * 2 + (r + 2), r)
                    scatter(i * 2 + r, r)
            for r in range(2):
                scatter(NB - 2 + r, r)

        @block.vector
        def _(dve):
            v = nc.vector
            done = [0]

            def step(ins):
                done[0] += 1
                ins.then_inc(s_v, 1)
                dve.wait_ge(s_v, done[0])

            for tile in (src_i, dst_i, ew):
                v.memset(tile[96:P, ELAST:EC], 0).then_inc(s_pad, 1)
            v.memset(xs[:, NT - 1, :], 0.0).then_inc(s_pad, 1)
            dve.wait_ge(s_const, 12)
            dve.wait_ge(s_edge, 96)
            step(v.tensor_scalar(tmp_i[:, :], src_i[:, :], SH, None, ALU.arith_shift_right))
            step(v.tensor_copy(bin_f[:, :], tmp_i[:, :]))
            for b in range(NT):
                last = v.tensor_scalar(inbin_v[:, b, :], bin_f[:, :], float(b), None, ALU.is_equal)
            step(last)
            for b in range(NT):
                last = v.tensor_tensor_scan(scan_v[:, b, :], ones_e[:, :], inbin_v[:, b, :], 0.0, ALU.mult, ALU.add)
            step(last)
            v.tensor_copy(cnt[:, :], scan_v[:, :, EC - 1]).then_inc(s_cnt, 1)

            def aggregate():
                for t in range(NT):
                    last = v.bn_aggr(mv[:, t, :], stats[:, t, :])
                last.then_inc(s_var, 1)

            def rstd(n):
                ve, r, a, nb = (ln[i][:, :] for i in range(4))
                dve.wait_ge(s_var, n)
                step(v.tensor_scalar(ve, mv[:, :, 1], EPS, None, ALU.add))
                dve.wait_ge(s_std, n)
                step(v.reciprocal(r, a))
                step(v.tensor_tensor(a, r, r, ALU.mult))
                step(v.tensor_tensor(a, a, ve, ALU.mult))
                step(v.tensor_scalar(a, a, -0.5, 1.5, ALU.mult, ALU.add))
                step(v.tensor_tensor(r, r, a, ALU.mult))
                v.scalar_tensor_tensor(nb, mv[:, :, 0], -1.0, r, ALU.mult, ALU.mult).then_inc(s_rstd, 1)

            dve.wait_ge(s_x, 32)
            for t in range(NT):
                last = v.bn_stats(stats[:, t, :], xs[:, t, :])
            step(last)
            aggregate()
            rstd(1)

            dve.wait_ge(s_off, 1)
            step(v.tensor_scalar(tot_i[:, :], bank[7][:, 64:64 + NT], float(P - 1), None, ALU.add))
            step(v.tensor_scalar(tot_i[:, :], tot_i[:, :], SH, None, ALU.arith_shift_right))
            step(v.tensor_copy(gfirst[:, :], tot_i[:, :]))
            step(v.tensor_tensor_scan(gend[:, :], ones_e[:, 0:NT], gfirst[:, :], 0.0, ALU.mult, ALU.add))
            step(v.tensor_tensor(gfirst[:, :], gend[:, :], gfirst[:, :], ALU.subtract))
            step(v.scalar_tensor_tensor(base[:, :], gfirst[:, :], float(P), bank[7][:, 0:NT], ALU.mult, ALU.add))
            v.tensor_scalar(base[:, :], base[:, :], -1.0, None, ALU.add).then_inc(s_first, 1)
            dve.wait_ge(s_first, 1)
            for b in range(NT):
                last = v.scalar_tensor_tensor(scan_v[:, b, :], scan_v[:, b, :], base[:, b:b + 1], inbin_v[:, b, :], ALU.add, ALU.mult)
            step(last)
            step(v.tensor_reduce(pos_f[:, :], scan_v.rearrange("p b c -> p c b"), AX.X, ALU.add))
            step(v.tensor_copy(tmp_i[:, :], pos_f[:, :]))
            step(v.tensor_scalar(tmp2_i[:, :], tmp_i[:, :], SH, None, ALU.arith_shift_right))
            step(v.tensor_scalar(tmp_i[:, :], tmp_i[:, :], P - 1, None, ALU.bitwise_and))
            v.tensor_copy(group_f[:, :], tmp2_i[:, :])
            step(v.tensor_copy(slot16[:, :], tmp_i[:, :]))
            step(v.tensor_scalar(tmp_i[:, :], src_i[:, :], P - 1, None, ALU.bitwise_and))
            v.tensor_copy(val16[0][:, :], tmp_i[:, :])
            v.tensor_scalar(val16[1][:, :], dst_i[:, :], float(-DOFF), None, ALU.add)
            step(v.tensor_copy(val16[2][:, :], ew[:, :]))
            step(v.tensor_tensor(pos_f[:, :], ew[:, :], val16[2][:, :], ALU.subtract))
            step(v.tensor_copy(val16[3][:, :], pos_f[:, :]))
            step(v.tensor_tensor(val16[4][:, :], pos_f[:, :], val16[3][:, :], ALU.subtract))

            dve.wait_ge(s_firstT, 1)
            step(v.tensor_copy(first_col[0:NT, :], bank[7][0:NT, 128:129]))
            v.tensor_scalar(reached[0:NT, :], groups16[0:NT, :], first_col[0:NT, :], None, ALU.is_ge).then_inc(s_reached, 1)
            dve.wait_ge(s_binrow, 1)
            v.tensor_scalar(bin_i[:, :], bank[6][:, 0:NG], -1.0, None, ALU.add)

            ats = [0]

            def onehots(c, k, r):
                dve.wait_ge(s_onehot_free, (k + 1) * UE)

                def over_slots(ap):
                    return ap[:, bass.ds(c, UE)].rearrange("p (s u) -> p s u", s=1).broadcast_to([P, P, UE])
                v.tensor_tensor(at_slot[:, r, :, :], slots16[:, :, :], over_slots(slot16), ALU.is_equal).then_inc(s_at, 1)
                for u in range(UE):
                    v.tensor_scalar(in_group[:, r, u, :], groups16[:, :], group_f[:, bass.ds(c + u, 1)], None, ALU.is_equal)
                dve.wait_ge(s_at, k + 1)
                for f in range(5):
                    o = put_v[:, r, f, :, :]
                    last = v.tensor_tensor(o.bitcast(f16) if f < 2 else o, at_slot[:, r, :, :], over_slots(val16[f]), ALU.mult)
                last.then_inc(s_onehot, 1)

            with dve.Fori(0, EC // UE // 2) as i:
                for r in range(2):
                    onehots(i * (2 * UE) + r * UE, i * 2 + r, r)
            onehots(EC - UE, EC // UE - 1, 0)

            dve.wait_ge(s_sorted, 1)
            v.memset(scan[:, 0:NT * D], 0.0).then_inc(s_acc, PR)
            v.tensor_scalar(node_i[:, :], bank[1][:, 0:NG], float(DOFF), None, ALU.add).then_inc(s_lists, 1)
            v.tensor_copy(slot_src[:, :], bank[0][:, 0:NG]).then_inc(s_lists, 1)
            v.tensor_copy(slot_ew[:, :], bank[2][:, 0:NG]).then_inc(s_lists, 1)
            dve.wait_ge(s_lists, 3)

            def matrix(g, j):
                dve.wait_ge(s_part, g + (RING - MR + 1))
                v.tensor_scalar(mat[:, j % MR, :], slots32[:, :], slot_src[:, bass.ds(g, 1)], slot_ew[:, bass.ds(g, 1)],
                                ALU.is_equal, ALU.mult).then_inc(s_mat, 1)

            def accumulate(g, j, tile):
                dve.wait_ge(s_part, g + (RING + 1))
                dve.wait_ge(s_acc, g + PR)
                v.tensor_tensor(side[:, tile, :], side[:, tile, :], bank[3 + j % PR][:, 0:D], ALU.add).then_inc(s_acc, 1)

            with dve.Fori(0, NG // RING) as i:
                tiles = []
                for j in range(RING):
                    if j % 8 == 0:
                        _, some = nc.values_load_multi_w_load_instructions(
                            bin_i[0:1, bass.ds(i * RING + j, 8)], engines=[DVE], min_val=0, max_val=NT - 1)
                        tiles += some
                    matrix(i * RING + j, j)
                    if j >= 2:
                        accumulate(i * RING + (j - 2), j - 2, bass.ds(tiles[j - 2], 1))
                for j in (RING - 2, RING - 1):
                    accumulate(i * RING + j, j, bass.ds(tiles[j], 1))

            dve.sem_inc(s_lk, 2)
            dve.sem_inc(s_x1, 6)

            def x1_tile(t, r):
                dve.wait_ge(s_slope, t + 1)
                both = lk[:, r, :, :].rearrange("p k d -> p (k d)")
                v.tensor_tensor(both, both, bank[(2, 7)[r]][:, :], ALU.max).then_inc(s_lk, 1)
                dve.wait_ge(s_lk, t + 3)
                v.tensor_tensor(xs[:, t, :], xs[:, t, :], lk[:, r, 0, :], ALU.add).then_inc(s_x1, 1)
                dve.wait_ge(s_x1, t * 3 + 7)
                v.tensor_tensor(xs[:, t, :], xs[:, t, :], lk[:, r, 1, :], ALU.add).then_inc(s_x1, 1)
                dve.wait_ge(s_x1, t * 3 + 8)
                v.bn_stats(stats[:, t, :], xs[:, t, :]).then_inc(s_x1, 1)

            with dve.Fori(0, NT // 2) as i:
                for r in range(2):
                    x1_tile(i * 2 + r, r)
            x1_tile(NT - 1, 0)
            dve.wait_ge(s_x1, 3 * NT + 6)
            aggregate()
            rstd(2)

            v.memset(y_last[:, :, :], 0.0).then_inc(s_ylast, 1)
            step(v.memset(pgroup_f[:, K * NT:], -1.0))
            step(v.memset(pslot16[:, K * NT:], 0.0))
            step(v.memset(ptok16[:, K * NT:], 0.0))
            step(v.memset(pk16[:, K * NT:], 0.0))
            for k in range(K):
                v.memset(pk16[:, k * NT:(k + 1) * NT], float(k + 1))
                last = v.tensor_copy(ptok16[:, k * NT:(k + 1) * NT], tokens[:, :])
            step(last)

            dve.wait_ge(s_logit, NT)

            def over_tiles(col):
                return col.rearrange("p (x t) -> p x t", t=1).broadcast_to([P, X, NT])

            def over_experts(row):
                return row.rearrange("p (x t) -> p x t", x=1).broadcast_to([P, X, NT])

            step(v.tensor_tensor(logits, bank[5][:, 0:NT * X].rearrange("p (t x) -> p x t", x=X), over_tiles(gateb[:, :]), ALU.add))
            for k in range(K):
                step(v.tensor_reduce(top[k][:, :], logits.rearrange("p x t -> p t x"), AX.X, ALU.max))
                step(v.tensor_tensor(is_top, logits, over_experts(top[k][:, :]), ALU.is_equal))
                step(v.tensor_tensor(is_top, is_top, experts[:, :, :], ALU.mult))
                step(v.tensor_reduce(pick[:, :], is_top.rearrange("p x t -> p t x"), AX.X, ALU.min))
                step(v.tensor_tensor(chosen[k], experts[:, :, :], over_experts(pick[:, :]), ALU.is_equal))
                if k == 0:
                    step(v.scalar_tensor_tensor(logits, chosen[k], -BIG, logits, ALU.mult, ALU.add))
                step(v.tensor_scalar(chosen[k][:, :, NT - 1], chosen[k][:, :, NT - 1], valid[:, :], None, ALU.mult))
            v.tensor_tensor(gain[1][:, :], top[1][:, :], top[0][:, :], ALU.subtract).then_inc(s_gap, 1)
            step(v.tensor_tensor(spread, chosen[0], chosen[1], ALU.add))
            for e in range(X):
                last = v.tensor_tensor_scan(rank[:, e, :], ones_e[:, 0:NT], spread[:, e, :], 0.0, ALU.mult, ALU.add)
            step(last)
            v.tensor_copy(bases[:, :], rank[:, :, NT - 1]).then_inc(s_bcnt, 1)
            dve.wait_ge(s_exp, 1)
            step(v.tensor_scalar(gain[0][:, :], gain[1][:, :], 1.0, None, ALU.add))
            step(v.reciprocal(gain[0][:, :], gain[0][:, :]))
            step(v.tensor_tensor(gain[1][:, :], gain[1][:, :], gain[0][:, :], ALU.mult))
            dve.wait_ge(s_boff, 1)
            step(v.tensor_scalar(btot_i[:, :], bank[6][:, 64:64 + X], float(BS - 1), None, ALU.add))
            step(v.tensor_scalar(btot_i[:, :], btot_i[:, :], BS.bit_length() - 1, None, ALU.arith_shift_right))
            step(v.tensor_copy(bfirst[:, :], btot_i[:, :]))
            step(v.tensor_tensor_scan(bend[:, :], ones_e[:, 0:X], bfirst[:, :], 0.0, ALU.mult, ALU.add))
            v.tensor_tensor(bfirst[:, :], bend[:, :], bfirst[:, :], ALU.subtract).then_inc(s_bfirst, 1)
            dve.wait_ge(s_bfirst, 1)
            step(v.scalar_tensor_tensor(bases[:, :], bfirst[:, :], float(BS), bank[6][:, 0:X], ALU.mult, ALU.add))
            step(v.tensor_tensor(rank, rank, over_tiles(bases[:, :]), ALU.add))
            for k in range(K):
                step(v.tensor_tensor(spread, rank, chosen[k], ALU.mult))
                step(v.tensor_reduce(place_f[:, k * NT:(k + 1) * NT], spread.rearrange("p x t -> p t x"), AX.X, ALU.add))
            step(v.tensor_scalar(place_i[:, 0:K * NT], place_f[:, 0:K * NT], -1.0, None, ALU.add))
            step(v.tensor_scalar(place2_i[:, 0:K * NT], place_i[:, 0:K * NT], SH, None, ALU.arith_shift_right))
            step(v.tensor_scalar(place_i[:, 0:K * NT], place_i[:, 0:K * NT], P - 1, None, ALU.bitwise_and))
            step(v.tensor_copy(pgroup_f[:, 0:K * NT], place2_i[:, 0:K * NT]))
            step(v.tensor_copy(pslot16[:, 0:K * NT], place_i[:, 0:K * NT]))
            dve.wait_ge(s_bfirstT, 1)
            step(v.tensor_copy(first_col[0:X, :], bank[7][0:X, 128:129]))
            v.tensor_scalar(breached[0:X, :], groups16[0:X, 0:NB], first_col[0:X, :], None, ALU.is_ge).then_inc(s_breached, 1)
            dve.wait_ge(s_brow, 1)
            v.tensor_scalar(expert_i[:, :], bank[7][:, 0:NB], -1.0, None, ALU.add).then_inc(s_blocks, 1)

            for n in range(NA // UE):
                r = n % 2
                if n >= 2:
                    dve.wait_ge(s_pfree, n - 1)
                c = slice(n * UE, (n + 1) * UE)

                def spread_over(ap):
                    return ap[:, c].rearrange("p (s u) -> p s u", s=1).broadcast_to([P, P, UE])
                v.tensor_tensor(at_slot[:, r, :, :], slots16[:, :, :], spread_over(pslot16), ALU.is_equal).then_inc(s_pat, 1)
                v.tensor_tensor(in_group[:, r, :, 0:NS], groups16[:, 0:NS].rearrange("p (u g) -> p u g", u=1).broadcast_to([P, UE, NS]),
                                pgroup_f[:, c].rearrange("p (u g) -> p u g", g=1).broadcast_to([P, UE, NS]), ALU.is_equal)
                dve.wait_ge(s_pat, n + 1)
                v.tensor_tensor(put_v[:, r, 0, :, :].bitcast(f16), at_slot[:, r, :, :], spread_over(ptok16), ALU.mult)
                v.tensor_tensor(put_v[:, r, 1, :, :].bitcast(f16), at_slot[:, r, :, :], spread_over(pk16), ALU.mult).then_inc(s_pone, 1)
            dve.wait_ge(s_placed, 1)
            step(v.tensor_scalar(empty_f[:, :], bank[1][:, 0:NS], 0.0, float(NOROW), ALU.is_equal, ALU.mult))
            step(v.tensor_tensor(empty_f[:, :], empty_f[:, :], bank[1][:, 0:NS], ALU.add))
            step(v.scalar_tensor_tensor(row_f[:, :], bank[0][:, 0:NS], float(K), empty_f[:, :], ALU.mult, ALU.add))
            v.tensor_scalar(row_i[:, :], row_f[:, :], float(K * DOFF - 1), None, ALU.add).then_inc(s_routes, 1)
            v.tensor_scalar(token_i[:, :], bank[0][:, 0:NS], float(DOFF), None, ALU.add).then_inc(s_routes, 1)

            v.tensor_tensor(xs[:, :, :], xs[:, :, :], bet[:, :].rearrange("p (t d) -> p t d", t=1).broadcast_to([P, NT, D]), ALU.add)

            dve.sem_inc(s_ysb, 4)
            with dve.Fori(0, NB // 2) as i:
                for r in range(2):
                    b = i * 2 + r
                    dve.wait_ge(s_y, b + 3)
                    dve.wait_ge(s_yout[r], i * 32)
                    for q in range(2):
                        v.tensor_copy(y_sb[:, r, q, :], bank[YB[r][q]][:, 0:D]).then_inc(s_ysb, 1)

            def ffn_sum(t, y, k0):
                tile = hs[:, bass.ds(t, 1), :].rearrange("p t d -> p (t d)")
                c = bass.ds(t, 1)
                v.scalar_tensor_tensor(tile, y[:, 0, :], gain[0][:, c], tile, ALU.mult, ALU.add).then_inc(s_sum, 1)
                dve.wait_ge(s_sum, k0 + 1)
                v.scalar_tensor_tensor(tile, y[:, 1, :], gain[1][:, c], tile, ALU.mult, ALU.add).then_inc(s_sum, 1)
                dve.wait_ge(s_sum, k0 + 2)
                v.bn_stats(stats[:, bass.ds(t, 1), :].rearrange("p t s -> p (t s)"), tile).then_inc(s_sum, 1)

            dve.sem_inc(s_sum, YR * 3)
            with dve.Fori(0, (NT - 1) // YR) as i:
                for j in range(YR):
                    dve.wait_ge(s_yin[j], i * 16 + 16)
                    ffn_sum(i * YR + j, y_in[:, j, :, :], (i * YR + (j + YR)) * 3)
            dve.wait_ge(s_ylast, 17)
            ffn_sum(NT - 1, y_last, (NT - 1 + YR) * 3)
            dve.wait_ge(s_sum, (NT + YR) * 3)
            aggregate()
            rstd(3)
            with dve.Fori(0, NT) as t:
                tile = hs[:, bass.ds(t, 1), :].rearrange("p t d -> p (t d)")
                dve.wait_ge(s_norm, t + 1)
                v.tensor_tensor(tile, tile, gam[:, :], ALU.mult).then_inc(s_fin, 1)
                dve.wait_ge(s_fin, t * 2 + 1)
                v.tensor_tensor(tile, tile, xs[:, bass.ds(t, 1), :].rearrange("p t d -> p (t d)"), ALU.add).then_inc(s_fin, 1)

        @block.scalar
        def _(act):
            a = nc.scalar
            act.wait_ge(s_const, 12)
            act.wait_ge(s_var, 1)

            def std(n):
                act.wait_ge(s_var, n)
                a.activation(ln[2][:, :], mv[:, :, 1], ACT.Sqrt, bias=eps_col[:, :]).then_inc(s_std, 1)
                act.wait_ge(s_rstd, n)

            def normalise(tiles, t, done):
                c = bass.ds(t, 1)
                a.activation(hs[:, c, :].rearrange("p t d -> p (t d)"), tiles[:, c, :].rearrange("p t d -> p (t d)"), ACT.Identity,
                             bias=ln[3][:, c], scale=ln[1][:, c]).then_inc(done, 1)

            std(1)
            with act.Fori(0, NT) as t:
                normalise(xs, t, s_h)

            def copy_T(t, r):
                act.wait_ge(s_uvT, t + 3)
                act.wait_ge(s_o, t + 1)
                a.activation(uvT[:, r, :, :].rearrange("p c n -> p (c n)"), bank[r][:, :], ACT.Copy).then_inc(s_uvTc, 1)

            def slope(t, r):
                act.wait_ge(s_o, t + 3)
                act.wait_ge(s_x1, t * 3 + 3)
                a.activation(lk[:, r, :, :].rearrange("p k d -> p (k d)"), bank[(2, 7)[r]][:, :], ACT.Copy, scale=SLOPE).then_inc(s_slope, 1)

            act.sem_inc(s_uvTc, 2)
            act.wait_ge(s_acc, NG + PR)
            copy_T(0, 0)
            with act.Fori(0, NT // 2) as i:
                for r in range(2):
                    copy_T(i * 2 + (r + 1), 1 - r)
                    slope(i * 2 + r, r)
            slope(NT - 1, 0)

            def copy_zT(t, r):
                act.wait_ge(s_zTg, t + 1)
                act.wait_ge(s_logit, t)
                a.activation(zTg[:, r, :, :].rearrange("p c n -> p (c n)"), bank[3 + r][:, 0:D], ACT.Copy).then_inc(s_zTgc, 1)

            act.sem_inc(s_zTgc, 2)
            std(2)
            normalise(xs, 0, s_z)
            with act.Fori(0, NT // 2) as i:
                for r in range(2):
                    normalise(xs, i * 2 + (r + 1), s_z)
                    copy_zT(i * 2 + r, r)
            copy_zT(NT - 1, 0)

            act.wait_ge(s_gap, 1)
            a.activation(gain[1][:, :], gain[1][:, :], ACT.Exp).then_inc(s_exp, 1)
            act.wait_ge(s_b1T, 1)
            a.activation(b1T[:, :], bank[4][:, 0:X * KF], ACT.Copy).then_inc(s_b1, 1)
            act.wait_ge(s_b1, 1)

            def copy_block(b, r):
                act.wait_ge(s_zgT, b + 3)
                act.wait_ge(s_hid, b * 2 + 2)
                a.activation(zT[:, r, :, :].rearrange("p c n -> p (c n)"), bank[1 + r][:, :], ACT.Copy).then_inc(s_zTc, 1)

            def relus(b, r, e):
                act.wait_ge(s_y, b + 1)
                for c in range(KF):
                    act.wait_ge(s_hid, b * 2 + (5 + c // 2))
                    a.activation(hT[:, r, c, :], bank[3 + c // 2][:, (c % 2) * BS:(c % 2 + 1) * BS], ACT.Relu,
                                 bias=b1T[:, bass.ds(e * KF + c, 1)]).then_inc(s_relu, 1)

            def block_experts(b):
                _, es = nc.values_load_multi_w_load_instructions(expert_i[0:1, bass.ds(b, 2)], engines=[ACTE], min_val=0, max_val=X - 1)
                return es

            act.wait_ge(s_blocks, 1)
            act.sem_inc(s_zTc, 2)
            act.sem_inc(s_relu, 4)
            copy_block(0, 0)
            with act.Fori(0, NB // 2 - 1) as i:
                es = block_experts(i * 2)
                for r in range(2):
                    copy_block(i * 2 + (r + 1), 1 - r)
                    relus(i * 2 + r, r, es[r])
            es = block_experts(NB - 2)
            copy_block(NB - 1, 1)
            relus(NB - 2, 0, es[0])
            relus(NB - 1, 1, es[1])

            std(3)
            with act.Fori(0, NT) as t:
                normalise(hs, t, s_norm)

        @block.tensor
        def _(pe):
            t_ = nc.tensor
            pe.wait_ge(s_const, 12)
            pe.wait_ge(s_cnt, 1)
            t_.matmul(bank[7][:, 0:NT], below[:, :], cnt[:, :], start=True, stop=True)
            t_.matmul(bank[7][:, 64:64 + NT], ones[:, :], cnt[:, :], start=True, stop=True).then_inc(s_off, 1)
            pe.wait_ge(s_first, 1)
            t_.matmul(bank[7][0:NT, 128:129], gfirst[0:1, :], ones[0:1, 0:1], start=True, stop=True).then_inc(s_firstT, 1)
            pe.wait_ge(s_reached, 1)
            t_.matmul(bank[6][:, 0:NG], ones_e[0:NT, 0:P], reached[0:NT, :], start=True, stop=True).then_inc(s_binrow, 1)

            for f in range(3):
                last = t_.matmul(bank[f][:, 0:NG], zeros16[:, 0:P], zeros16[:, 0:NG], start=True, stop=False)
            last.then_inc(s_onehot_free, 2 * UE)

            def sort(k, r):
                pe.wait_ge(s_onehot, k + 1)
                for u in range(UE):
                    for f in range(5):
                        o = put_v[:, r, f, :, u]
                        last = t_.matmul(bank[min(f, 2)][:, 0:NG], o.bitcast(f16) if f < 2 else o, in_group[:, r, u, :], start=False, stop=False)
                    last.then_inc(s_onehot_free, 1)

            with pe.Fori(0, EC // UE // 2) as i:
                for r in range(2):
                    sort(i * 2 + r, r)
            sort(EC // UE - 1, 0)
            for f in range(3):
                last = t_.matmul(bank[f][:, 0:NG], zeros16[:, 0:P], zeros16[:, 0:NG], start=False, stop=True)
            last.then_inc(s_sorted, 1)

            pe.sem_inc(s_part, RING)
            with pe.Fori(0, NG // RING) as i:
                for j in range(RING):
                    g = i * RING + j
                    pe.wait_ge(s_mat, g + 1)
                    pe.wait_ge(s_acc, g + 1)
                    pe.wait_ge(s_got[j], i * 16 + 16)
                    t_.matmul(bank[3 + j % PR][:, 0:D], mat[:, j % MR, :], ring[:, j, :], start=True, stop=True).then_inc(s_part, 1)

            def transposes(t, r):
                pe.wait_ge(s_uv, t + 1)
                pe.wait_ge(s_uvTc, t + 1)
                for k in range(2):
                    for c in range(KD):
                        q = k * KD + c
                        last = t_.transpose(bank[r][:, q * P:(q + 1) * P], uv[:, r, k, c * P:(c + 1) * P], ident[:, :])
                last.then_inc(s_uvT, 1)

            def products(t, r):
                pe.wait_ge(s_uvTc, t + 3)
                pe.wait_ge(s_lk, t + 1)
                o = bank[(2, 7)[r]]
                for k in range(2):
                    last = t_.matmul(o[:, k * D:(k + 1) * D], ones[0:1, :], gb[:, k, :], start=True, stop=False)
                    for c in range(KD):
                        last = t_.matmul(o[:, k * D:(k + 1) * D], uvT[:, r, k * KD + c, :], gw[:, k, c, :], start=False, stop=c == KD - 1)
                last.then_inc(s_o, 1)

            pe.wait_ge(s_wload, 144)
            pe.sem_inc(s_uvT, 2)
            pe.sem_inc(s_o, 2)
            transposes(0, 0)
            with pe.Fori(0, NT // 2) as i:
                for r in range(2):
                    transposes(i * 2 + (r + 1), 1 - r)
                    products(i * 2 + r, r)
            products(NT - 1, 0)

            def gate_transposes(t, r):
                pe.wait_ge(s_z, t + 1)
                pe.wait_ge(s_zTgc, t + 1)
                for c in range(KD):
                    last = t_.transpose(bank[3 + r][:, c * P:(c + 1) * P], hs[:, bass.ds(t, 1), c * P:(c + 1) * P].rearrange("p t d -> p (t d)"), ident[:, :])
                last.then_inc(s_zTg, 1)

            def gate_products(t, r):
                pe.wait_ge(s_zTgc, t + 3)
                for c in range(KD):
                    last = t_.matmul(bank[5][:, bass.ds(t * X, X)], zTg[:, r, c, :], gatew[:, c, :], start=c == 0, stop=c == KD - 1)
                last.then_inc(s_logit, 1)

            gate_transposes(0, 0)
            for t in range(NT):
                if t + 1 < NT:
                    gate_transposes(t + 1, 1 - t % 2)
                gate_products(t, t % 2)

            pe.wait_ge(s_bcnt, 1)
            t_.matmul(bank[6][:, 0:X], below[:, :], bases[:, :], start=True, stop=True)
            t_.matmul(bank[6][:, 64:64 + X], ones[:, :], bases[:, :], start=True, stop=True).then_inc(s_boff, 1)
            t_.transpose(bank[4][:, 0:X * KF], b1_rows[:, :], ident[0:X * KF, 0:X * KF]).then_inc(s_b1T, 1)
            pe.wait_ge(s_bfirst, 1)
            t_.matmul(bank[7][0:X, 128:129], bfirst[0:1, :], ones[0:1, 0:1], start=True, stop=True).then_inc(s_bfirstT, 1)
            pe.wait_ge(s_breached, 1)
            t_.matmul(bank[7][:, 0:NB], ones_e[0:X, 0:P], breached[0:X, :], start=True, stop=True).then_inc(s_brow, 1)

            for n in range(NA // UE):
                pe.wait_ge(s_pone, n + 1)
                for u in range(UE):
                    for f in range(2):
                        last = t_.matmul(bank[f][:, 0:NS], put_v[:, n % 2, f, :, u].bitcast(f16), in_group[:, n % 2, u, 0:NS],
                                         start=n == 0 and u == 0, stop=n == NA // UE - 1 and u == UE - 1)
                last.then_inc(s_pfree, 1)
            pe.wait_ge(s_pfree, NA // UE)
            pe.sem_inc(s_placed, 1)

            def block_transposes(b, i, r):
                for q in range(2):
                    pe.wait_ge(s_zg[r * 2 + q], i * 16 + 16)
                pe.wait_ge(s_zTc, b + 1)
                for c in range(KD):
                    for q in range(2):
                        last = t_.transpose(bank[1 + r][:, c * BS + q * P:c * BS + (q + 1) * P], zg[:, r, q, c * P:(c + 1) * P], ident[:, :])
                last.then_inc(s_zgT, 1)

            def block(b, i, r):
                pe.wait_ge(s_w[r], i * 48 + 48)
                pe.wait_ge(s_zTc, b + 3)
                for c in range(KF):
                    pe.wait_ge(s_relu, b * 4 + (c // 2 * 2 + 2))
                    for k in range(KD):
                        last = t_.matmul(bank[3 + c // 2][:, (c % 2) * BS:(c % 2 + 1) * BS], w1_sb[:, r, k, c * P:(c + 1) * P], zT[:, r, k, :],
                                         start=k == 0, stop=k == KD - 1)
                    if c % 2:
                        last.then_inc(s_hid, 1)
                pe.wait_ge(s_ysb, b * 2 + 2)
                for q in range(2):
                    t_.matmul(bank[YB[r][q]][:, 0:D], ones[0:1, :], b2_sb[:, r, :], start=True, stop=False)
                for c in range(KF):
                    pe.wait_ge(s_relu, b * 4 + (c + 5))
                    for q in range(2):
                        last = t_.matmul(bank[YB[r][q]][:, 0:D], hT[:, r, c, q * P:(q + 1) * P], w2_sb[:, r, c, :], start=False, stop=c == KF - 1)
                last.then_inc(s_y, 1)

            pe.wait_ge(s_b1, 1)
            pe.sem_inc(s_zgT, 2)
            pe.sem_inc(s_hid, 4)
            pe.sem_inc(s_y, 2)
            block_transposes(0, 0, 0)
            with pe.Fori(0, NB // 2 - 1) as i:
                for r in range(2):
                    block_transposes(i * 2 + (r + 1), i + r, 1 - r)
                    block(i * 2 + r, i, r)
            block_transposes(NB - 1, NB // 2 - 1, 1)
            block(NB - 2, NB // 2 - 1, 0)
            block(NB - 1, NB // 2 - 1, 1)


_INS = ['x', 'src', 'dst', 'edge_weight', 'L0_gnn_W1', 'L0_gnn_b1', 'L0_gnn_W2', 'L0_gnn_b2', 'L0_ffn_gate_w',
        'L0_ffn_gate_b', 'L0_ffn_w1', 'L0_ffn_b1', 'L0_ffn_w2', 'L0_ffn_b2', 'L0_ffn_gamma', 'L0_ffn_beta']


def kernel(**inputs):
    import numpy as np
    import concourse.bacc as bacc
    from concourse.bass_utils import run_bass_kernel_spmd as run

    nc = bacc.Bacc("TRN2", target_bir_lowering=False, num_devices=1)
    arrays, args = {}, []
    for name in _INS:
        a = np.ascontiguousarray(inputs[name])
        arrays[f"in_{name}"] = a
        args.append(nc.dram_tensor(f"in_{name}", a.shape, mybir.dt.from_np(a.dtype), kind="ExternalInput").ap())
    args.append(nc.dram_tensor("out_x", (N, D), f32, kind="ExternalOutput").ap())
    build(nc, *args)
    return run(nc, [arrays], core_ids=[0]).results[0]["out_x"]
```

```python
import concourse.bass as bass
from concourse import mybir
from contextlib import ExitStack

f32 = mybir.dt.float32
bf16 = mybir.dt.bfloat16
f16 = mybir.dt.float16
i32 = mybir.dt.int32
ALU = mybir.AluOpType
ACT = mybir.ActivationFunctionType
AX = mybir.AxisListType
DVE = mybir.EngineType.DVE
SP = mybir.EngineType.SP
ACTE = mybir.EngineType.Activation

P = 128
SH = 7
N, D = 3125, 256
KD = D // P
E = 50000
NT = -(-N // P)
BROWS = 65
WLOADS = 2 + 2 * 3 + 1 + 3 + 1
LAST = N - (NT - 1) * P
UE = 8
EC = -(-E // P // UE) * UE
ELAST = E - (P - 1) * EC
BATCHES = (-(-EC // UE // 2), EC // UE // 2)
PCOL = (0, BATCHES[0] * UE)
PEND = (PCOL[1], EC)
NGP = tuple((UE * b * P + NT * (P - 1)) // P for b in BATCHES)
NG = sum(NGP)
PG = (0, NGP[0])
DOFF = N // 2
TURN = 8
RING = 2 * TURN
AHEAD = 4
PR = 4
X, F, K = 16, 512, 2
KF = F // P
BS = 256
NB = (K * N + X * (BS - 1)) // BS
LASTPAIR = (-(-K * N // BS) + 1) // 2 - 1, NB // 2 - 1
NS = NB * (BS // P)
NA = -(-K * NT // UE) * UE
NOROW = 8192
BIG = 3.0e38
YR = 8
EPS = 1e-5
SLOPE = 0.01

assert NGP[0] % RING == 0 and NGP[1] % RING == TURN and BATCHES[0] % 2 == 1 and BATCHES[1] % 2 == 0
assert BATCHES[1] < NGP[0] // TURN and UE == TURN
assert NT % 2 == 1 and NB % 2 == 0 and 0 < ELAST <= EC
assert (NT - 1) % YR == 0 and K * NT < NA and 2 * (DOFF + 1) < NOROW


def build(nc, x, src, dst, edge_weight, gW1, gb1, gW2, gb2, gate_w, gate_b, w1, b1, w2, b2, gamma, beta, out):
    h_dram = nc.dram_tensor("h_dram", (NT * P, D), f32).ap()
    z_dram = nc.dram_tensor("z_dram", (NT * P, D), f32).ap()
    y_dram = nc.dram_tensor("y_dram", (NT * P * K, D), f32).ap()

    with ExitStack() as ctx:
        def sb(name, shape, dt=f32):
            return ctx.enter_context(nc.sbuf_tensor(name, shape, dt))

        def sem(name):
            return ctx.enter_context(nc.semaphore(name))

        bank = [ctx.enter_context(nc.psum_tensor(f"bank{i}", [P, 512], f32)) for i in range(8)]

        slots16 = sb("slots16", [P, P, UE], f16)
        slots32 = sb("slots32", [P, P])
        groups16 = sb("groups16", [P, NGP[0]], f16)
        below = sb("below", [P, P])
        ones = sb("ones", [P, P])
        ident = sb("ident", [P, P])
        zeros16 = sb("zeros16", [P, NGP[0]], bf16)
        eps_col = sb("eps_col", [P, 1])
        tokens = sb("tokens", [P, NT])
        valid = sb("valid", [P, 1])
        experts = sb("experts", [P, X, NT])

        xs = sb("xs", [P, NT, D])
        hs = sb("hs", [P, NT, D])
        stats = sb("stats", [P, NT, 6])
        mv = sb("mv", [P, NT, 2])
        ln = [sb(f"ln{i}", [P, NT]) for i in range(4)]

        src_i = sb("src_i", [P, EC], i32)
        dst_i = sb("dst_i", [P, EC], i32)
        ew = sb("ew", [P, EC])
        bin_f = sb("bin_f", [P, EC])
        tmp_i = sb("tmp_i", [P, EC], i32)
        tmp2_i = sb("tmp2_i", [P, EC], i32)
        pos_f = sb("pos_f", [P, EC])
        group_f = sb("group_f", [P, EC])
        slot16 = sb("slot16", [P, EC], f16)
        val16 = [sb(f"val16_{i}", [P, EC], f16 if i < 2 else bf16) for i in range(5)]
        inbin = sb("inbin", [P, NT * EC], bf16)
        scan = sb("scan", [P, NT * EC])
        inbin_v = inbin[:, :].rearrange("p (b c) -> p b c", c=EC)
        scan_v = scan[:, :].rearrange("p (b c) -> p b c", c=EC)
        ones_e = sb("ones_e", [P, EC], bf16)
        cnt = sb("cnt", [P, 2 * NT])
        base = sb("base", [P, 2 * NT])
        tot_i = sb("tot_i", [P, 2 * NT], i32)
        gend = sb("gend", [P, 2 * NT])
        gfirst = sb("gfirst", [P, 2 * NT])
        first_col = sb("first_col", [P, 1])
        first_cols = sb("first_cols", [P, 2])
        reached = sb("reached", [P, NG], bf16)
        bin_i = sb("bin_i", [P, NG], i32)
        at_slot = sb("at_slot", [P, 2, P, UE], bf16)
        put = sb("put", [P, 2, 5, P * UE], bf16)
        put_v = put[:, :, :, :].rearrange("p r f (s u) -> p r f s u", u=UE)
        in_group = sb("in_group", [P, 2, UE, NGP[0]], bf16)

        node_i = sb("node_i", [P, NG], i32)
        slot_src = sb("slot_src", [P, NG + AHEAD])
        slot_ew = sb("slot_ew", [P, NG + AHEAD])
        stage = sb("stage", [P, 4, 4], i32)
        ring = sb("ring", [P, RING, D])
        mat = sb("mat", [P, TURN, P])
        side = scan[:, 0:NT * D].rearrange("p (t d) -> p t d", d=D)
        free0 = NT * D
        uv = scan[:, free0:free0 + 4 * D].rearrange("p (r k d) -> p r k d", r=2, k=2)
        uvT = scan[:, free0 + 4 * D:free0 + 8 * D].rearrange("p (r c n) -> p r c n", r=2, c=4)
        lk = scan[:, free0 + 8 * D:free0 + 12 * D].rearrange("p (r k d) -> p r k d", r=2, k=2)
        gw = sb("gw", [P, 2, KD, D])
        gb = sb("gb", [P, 2 * D])
        gb16 = inbin[0:BROWS, 0:2 * D]
        gatew = sb("gatew", [P, KD, X])
        gateb = sb("gateb", [P, X])

        YB = ((5, 6), (7, 0))
        at = [0]

        def part(*shape):
            n = 1
            for k in shape:
                n *= k
            at[0] += n
            assert at[0] <= NT * EC
            names = " ".join("abcd"[:len(shape)])
            view = scan[:, at[0] - n:at[0]]
            return view.rearrange(f"p ({names}) -> p {names}", **dict(zip("abcd", shape))) if len(shape) > 1 else view

        logits = part(X, NT)
        is_top = part(X, NT)
        chosen = [part(X, NT) for _ in range(K)]
        rank = part(X, NT)
        spread = part(X, NT)
        zTg = part(2, KD, P)
        y_sb = part(2, 2, D)
        y_in = part(YR, K, D)
        y_last = part(K, D)
        top = [sb(f"top{k}", [P, NT]) for k in range(K)]
        pick = sb("pick", [P, NT])
        gain = [sb(f"gain{k}", [P, NT]) for k in range(K)]
        bases = sb("bases", [P, X])
        btot_i = sb("btot_i", [P, X], i32)
        bfirst = sb("bfirst", [P, X])
        bend = sb("bend", [P, X])
        place_f = sb("place_f", [P, NA])
        place_i = sb("place_i", [P, NA], i32)
        place2_i = sb("place2_i", [P, NA], i32)
        pgroup_f = sb("pgroup_f", [P, NA])
        pslot16 = sb("pslot16", [P, NA], f16)
        ptok16 = sb("ptok16", [P, NA], f16)
        pk16 = sb("pk16", [P, NA], f16)
        breached = sb("breached", [P, NB], bf16)
        expert_i = sb("expert_i", [P, NB], i32)
        pair_i = sb("pair_i", [P, 1], i32)
        row_f = sb("row_f", [P, NS])
        empty_f = sb("empty_f", [P, NS])
        row_i = sb("row_i", [P, NS], i32)
        token_i = sb("token_i", [P, NS], i32)
        tstage = sb("tstage", [P, 2, 2], i32)
        rstage = sb("rstage", [P, 2, 2], i32)
        wring = inbin[:, 0:2 * 2 * 2 * KD * F].bitcast(f32).rearrange("p (r w n) -> p r w n", r=2, w=2)
        w1_sb = wring[:, :, 0, :].rearrange("p r (c f) -> p r c f", c=KD)
        w2_sb = wring[:, :, 1, :].rearrange("p r (c d) -> p r c d", c=KF)
        b2_sb = part(2, D)
        b1_rows = sb("b1_rows", [X * KF, P])
        b1T = sb("b1T", [P, X * KF])
        gam = sb("gam", [P, D])
        bet = sb("bet", [P, D])
        work = put[:, :, :, :].rearrange("p a b c -> p (a b c)").bitcast(f32)
        zg = work[:, 0:4 * D].rearrange("p (r s d) -> p r s d", r=2, s=2)
        zT = work[:, 4 * D:8 * D].rearrange("p (r c n) -> p r c n", r=2, c=KD)
        hT = work[:, 8 * D:16 * D].rearrange("p (r c n) -> p r c n", r=2, c=KF)

        s_const = sem("s_const")
        s_pad = sem("s_pad")
        s_edge = sem("s_edge")
        s_x = sem("s_x")
        s_wload = sem("s_wload")
        s_v = sem("s_v")
        s_cnt = sem("s_cnt")
        s_off = sem("s_off")
        s_var = sem("s_var")
        s_std = sem("s_std")
        s_rstd = sem("s_rstd")
        s_h = sem("s_h")
        s_htable = sem("s_htable")
        s_first = sem("s_first")
        s_firstT = sem("s_firstT")
        s_reached = sem("s_reached")
        s_binrow = sem("s_binrow")
        s_at = sem("s_at")
        s_onehot = sem("s_onehot")
        s_onehot_free = sem("s_onehot_free")
        s_sorted = sem("s_sorted")
        s_lists = sem("s_lists")
        s_stage = sem("s_stage")
        s_turn = sem("s_turn")
        s_got = [sem(f"s_got{i}") for i in range(RING)]
        s_mat = sem("s_mat")
        s_part = sem("s_part")
        s_acc = sem("s_acc")
        s_gb = sem("s_gb")
        s_uv = sem("s_uv")
        s_uvT = sem("s_uvT")
        s_uvTc = sem("s_uvTc")
        s_o = sem("s_o")
        s_lk = sem("s_lk")
        s_slope = sem("s_slope")
        s_x1 = sem("s_x1")
        s_z = sem("s_z")
        s_ztable = sem("s_ztable")
        s_zTg = sem("s_zTg")
        s_zTgc = sem("s_zTgc")
        s_logit = sem("s_logit")
        s_gap = sem("s_gap")
        s_exp = sem("s_exp")
        s_bcnt = sem("s_bcnt")
        s_boff = sem("s_boff")
        s_bfirst = sem("s_bfirst")
        s_bfirstT = sem("s_bfirstT")
        s_breached = sem("s_breached")
        s_brow = sem("s_brow")
        s_blocks = sem("s_blocks")
        s_b1T = sem("s_b1T")
        s_b1 = sem("s_b1")
        s_pat = sem("s_pat")
        s_pone = sem("s_pone")
        s_pfree = sem("s_pfree")
        s_placed = sem("s_placed")
        s_routes = sem("s_routes")
        s_tstage = sem("s_tstage")
        s_rstage = sem("s_rstage")
        s_zg = [sem(f"s_zg{i}") for i in range(4)]
        s_w = [sem(f"s_w{i}") for i in range(2)]
        s_bias = [sem(f"s_bias{i}") for i in range(2)]
        s_zgT = sem("s_zgT")
        s_zTc = sem("s_zTc")
        s_hid = sem("s_hid")
        s_relu = sem("s_relu")
        s_y = sem("s_y")
        s_ysb = sem("s_ysb")
        s_yout = [sem(f"s_yout{i}") for i in range(2)]
        s_yin = [sem(f"s_yin{i}") for i in range(YR)]
        s_ylast = sem("s_ylast")
        s_sum = sem("s_sum")
        s_norm = sem("s_norm")
        s_fin = sem("s_fin")
        s_out = sem("s_out")

        nodes_v = slice(0, (NT - 1) * P)

        def tiled(dram):
            return dram[nodes_v, :].rearrange("(t p) d -> p t d", p=P)

        def last_pair(engine):
            _, (n,) = nc.values_load_multi_w_load_instructions(pair_i[0:1, 0:1], engines=[engine], min_val=LASTPAIR[0], max_val=LASTPAIR[1])
            return n

        block = ctx.enter_context(nc.Block())

        @block.sync
        def _(sp):
            sp.wait_ge(s_pad, 5)
            for tile, dram in ((src_i, src), (dst_i, dst), (ew, edge_weight)):
                sp.dma_start(tile[0:P - 1, :], dram[0:(P - 1) * EC].rearrange("(p c) -> p c", c=EC)).then_inc(s_edge, 16)
                sp.dma_start(tile[P - 1:P, 0:ELAST], dram[(P - 1) * EC:E].rearrange("(p c) -> p c", p=1)).then_inc(s_edge, 16)
            sp.dma_start(xs[:, 0:NT - 1, :], tiled(x)).then_inc(s_x, 16)
            sp.dma_start(xs[0:LAST, NT - 1, :], x[(NT - 1) * P:N, :]).then_inc(s_x, 16)
            for k, (w, b) in enumerate(((gW1, gb1), (gW2, gb2))):
                sp.dma_start(gw[:, k, :, :], w.rearrange("(c p) n -> p c n", p=P)).then_inc(s_wload, 16)
                for row in range(0, BROWS, 32):
                    sp.dma_start(gb[row:row + 1, k * D:(k + 1) * D], b.rearrange("(a n) -> a n", a=1)).then_inc(s_wload, 16)
            sp.dma_start(gatew[:, :, :], gate_w.rearrange("(c p) n -> p c n", p=P)).then_inc(s_wload, 16)
            for tile, dram in ((gateb, gate_b), (gam, gamma), (bet, beta)):
                sp.dma_start(tile[:, :], dram.rearrange("(a n) -> a n", a=1).broadcast_to(tile.shape)).then_inc(s_wload, 16)
            sp.dma_start(b1_rows[:, :], b1.rearrange("x (c p) -> (x c) p", p=P)).then_inc(s_wload, 16)
            sp.wait_ge(s_h, NT)
            sp.dma_start(h_dram.rearrange("(t p) d -> p t d", p=P), hs[:, :, :]).then_inc(s_htable, 16)
            sp.wait_ge(s_z, NT)
            sp.dma_start(z_dram.rearrange("(t p) d -> p t d", p=P), hs[:, :, :]).then_inc(s_ztable, 16)

            sp.wait_ge(s_blocks, 1)
            end = last_pair(SP)
            with sp.Fori(0, end + 1) as i:
                _, es = nc.values_load_multi_w_load_instructions(expert_i[0:1, bass.ds(i * 2, 2)], engines=[SP], min_val=0, max_val=X - 1)
                for r in range(2):
                    e = bass.ds(es[r], 1)
                    sp.wait_ge(s_y, i * 2 + (r + 1))
                    sp.dma_start(w1_sb[:, r, :, :], w1[e, :, :].rearrange("x (c p) f -> p (x c) f", p=P)).then_inc(s_w[r], 16)
                    sp.dma_start(w2_sb[:, r, :, :], w2[e, :, :].rearrange("x (c p) d -> p (x c) d", p=P)).then_inc(s_w[r], 16)
                    sp.wait_ge(s_ysb, i * 4 + (2 * r + 2))
                    sp.dma_start(b2_sb[:, r, :], b2[e, :].broadcast_to([P, D])).then_inc(s_bias[r], 16)

            for r in range(2):
                sp.wait_ge(s_yout[r], end * 32 + 32)
            y_rows = y_dram.rearrange("(t p k) d -> t p k d", p=P, k=K)
            sp.dma_start(y_last[0:LAST, :, :], y_rows[NT - 1, 0:LAST, :, :]).then_inc(s_ylast, 16)
            with sp.Fori(0, (NT - 1) // YR) as i:
                for j in range(YR):
                    sp.wait_ge(s_sum, (i * YR + j + 1) * 3)
                    sp.dma_start(y_in[:, j, :, :], y_rows[bass.ds(i * YR + j, 1), :, :, :].rearrange("t p k d -> (t p) k d")).then_inc(s_yin[j], 16)

            with sp.Fori(0, NT - 1) as t:
                sp.wait_ge(s_fin, t * 2 + 2)
                sp.dma_start(out[bass.ds(t * P, P), :], hs[:, bass.ds(t, 1), :].rearrange("p t d -> p (t d)")).then_inc(s_out, 16)
            sp.wait_ge(s_fin, NT * 2)
            sp.dma_start(out[(NT - 1) * P:N, :], hs[0:LAST, NT - 1, :]).then_inc(s_out, 16)
            sp.wait_ge(s_out, NT * 16)

        @block.gpsimd
        def _(gp):
            made = [0]

            def const(ins):
                made[0] += 1
                ins.then_inc(s_const, 1)
                gp.wait_ge(s_const, made[0])

            const(gp.iota(slots16[:, :, :], pattern=[[1, P], [0, UE]], base=0, channel_multiplier=0, allow_small_or_imprecise_dtypes=True))
            const(gp.iota(slots32[:, :], pattern=[[1, P]], base=0, channel_multiplier=0, allow_small_or_imprecise_dtypes=True))
            const(gp.iota(groups16[:, :], pattern=[[1, NGP[0]]], base=0, channel_multiplier=0, allow_small_or_imprecise_dtypes=True))
            const(gp.memset(ones[:, :], 1.0))
            const(gp.memset(ones_e[:, :], 1.0))
            const(gp.memset(zeros16[:, :], 0.0))
            const(gp.memset(eps_col[:, :], EPS))
            const(gp.affine_select(out=below[:, :], in_=ones[:, :], compare_op=ALU.is_gt, fill=0.0, base=0,
                                   pattern=[[1, P]], channel_multiplier=-1))
            const(gp.affine_select(out=ident[:, :], in_=ones[:, :], compare_op=ALU.is_equal, fill=0.0, base=0,
                                   pattern=[[1, P]], channel_multiplier=-1))
            const(gp.affine_select(out=valid[:, :], in_=ones[:, 0:1], compare_op=ALU.is_gt, fill=0.0, base=LAST,
                                   pattern=[[0, 1]], channel_multiplier=-1))
            const(gp.iota(experts[:, :, :], pattern=[[1, X], [0, NT]], base=-X, channel_multiplier=0, allow_small_or_imprecise_dtypes=True))

            const(gp.iota(tokens[:, :], pattern=[[P, NT]], base=-DOFF, channel_multiplier=1, allow_small_or_imprecise_dtypes=True))

            def turn(n, r):
                for part4 in range(2 * r, 2 * r + 2):
                    g = n * TURN + (part4 - 2 * r) * 4
                    gp.wait_ge(s_part, g + 4)
                    gp.tensor_copy(stage[:, part4, :], node_i[:, bass.ds(g, 4)]).then_inc(s_stage, 1)
                    gp.wait_ge(s_stage, n * 2 + (part4 - 2 * r + 1))
                    gp.sem_inc(s_turn, 1)
                    for j in range(4):
                        slot = part4 * 4 + j
                        gp.indirect_dma_start(ring[:, slot, :], None, h_dram,
                                              bass.IndirectOffsetOnAxis(stage[:, part4, j:j + 1], 0)).then_inc(s_got[slot], 16)

            gp.wait_ge(s_htable, 16)
            for q in range(2):
                gp.wait_ge(s_lists, 3 * q + 1)
                with gp.Fori(PG[q] // RING, (PG[q] + NGP[q]) // RING) as i:
                    for r in range(2):
                        turn(i * 2 + r, r)
            turn(NG // TURN - 1, 0)

            gp.wait_ge(s_acc, NG + PR)
            def uv_tile(t, r):
                gp.wait_ge(s_uvT, t + 1)
                gp.tensor_tensor(uv[:, r, 0, :], hs[:, t, :], side[:, t, :], ALU.add)
                gp.tensor_tensor(uv[:, r, 1, :], hs[:, t, :], side[:, t, :], ALU.mult).then_inc(s_uv, 1)

            with gp.Fori(0, NT // 2) as i:
                for r in range(2):
                    uv_tile(i * 2 + r, r)
            uv_tile(NT - 1, 0)

            gp.wait_ge(s_routes, 2)
            gp.wait_ge(s_ztable, 16)

            def gather(b, r):
                gp.wait_ge(s_zgT, b + 1)
                gp.tensor_copy(tstage[:, r, :], token_i[:, bass.ds(b * 2, 2)]).then_inc(s_tstage, 1)
                gp.wait_ge(s_tstage, b + 1)
                gp.sem_inc(s_turn, 1)
                for q in range(2):
                    gp.indirect_dma_start(zg[:, r, q, :], None, z_dram, bass.IndirectOffsetOnAxis(tstage[:, r, q:q + 1], 0)).then_inc(s_zg[r * 2 + q], 16)

            def scatter(b, r):
                gp.wait_ge(s_ysb, b * 2 + 6)
                gp.tensor_copy(rstage[:, r, :], row_i[:, bass.ds(b * 2, 2)]).then_inc(s_rstage, 1)
                gp.wait_ge(s_rstage, b + 1)
                gp.sem_inc(s_turn, 1)
                for q in range(2):
                    gp.indirect_dma_start(y_dram, bass.IndirectOffsetOnAxis(rstage[:, r, q:q + 1], 0), y_sb[:, r, q, :], None,
                                          bounds_check=K * N - 1, oob_is_err=False).then_inc(s_yout[r], 16)

            for r in range(2):
                gather(r, r)
            end = last_pair(mybir.EngineType.Pool)
            with gp.Fori(0, end) as i:
                for r in range(2):
                    gather(i * 2 + (r + 2), r)
                    scatter(i * 2 + r, r)
            for r in range(2):
                scatter(end * 2 + r, r)

        @block.vector
        def _(dve):
            v = nc.vector
            done = [0]

            def step(ins):
                done[0] += 1
                ins.then_inc(s_v, 1)
                dve.wait_ge(s_v, done[0])

            for tile in (src_i, dst_i, ew):
                v.memset(tile[96:P, ELAST:EC], 0).then_inc(s_pad, 1)
            v.memset(xs[:, NT - 1, :], 0.0).then_inc(s_pad, 1)
            v.memset(gb[:, :], 0.0).then_inc(s_pad, 1)
            dve.wait_ge(s_const, 12)
            dve.wait_ge(s_edge, 96)
            step(v.tensor_scalar(tmp_i[:, :], src_i[:, :], SH, None, ALU.arith_shift_right))
            step(v.tensor_copy(bin_f[:, :], tmp_i[:, :]))
            for b in range(NT):
                last = v.tensor_scalar(inbin_v[:, b, :], bin_f[:, :], float(b), None, ALU.is_equal)
            step(last)
            for q in range(2):
                c = slice(PCOL[q], PEND[q])
                for b in range(NT):
                    last = v.tensor_tensor_scan(scan_v[:, b, c], ones_e[:, c], inbin_v[:, b, c], 0.0, ALU.mult, ALU.add)
            step(last)
            for q in range(2):
                last = v.tensor_copy(cnt[:, q * NT:(q + 1) * NT], scan_v[:, :, PEND[q] - 1])
            last.then_inc(s_cnt, 1)

            def aggregate():
                for t in range(NT):
                    last = v.bn_aggr(mv[:, t, :], stats[:, t, :])
                last.then_inc(s_var, 1)

            def rstd(n):
                ve, r, a, nb = (ln[i][:, :] for i in range(4))
                dve.wait_ge(s_var, n)
                step(v.tensor_scalar(ve, mv[:, :, 1], EPS, None, ALU.add))
                dve.wait_ge(s_std, n)
                step(v.reciprocal(r, a))
                step(v.tensor_tensor(a, r, r, ALU.mult))
                step(v.tensor_tensor(a, a, ve, ALU.mult))
                step(v.tensor_scalar(a, a, -0.5, 1.5, ALU.mult, ALU.add))
                step(v.tensor_tensor(r, r, a, ALU.mult))
                v.scalar_tensor_tensor(nb, mv[:, :, 0], -1.0, r, ALU.mult, ALU.mult).then_inc(s_rstd, 1)

            dve.wait_ge(s_x, 32)
            for t in range(NT):
                last = v.bn_stats(stats[:, t, :], xs[:, t, :])
            step(last)
            aggregate()
            rstd(1)

            dve.wait_ge(s_off, 1)
            step(v.tensor_scalar(tot_i[:, :], bank[7][:, 64:64 + 2 * NT], float(P - 1), None, ALU.add))
            step(v.tensor_scalar(tot_i[:, :], tot_i[:, :], SH, None, ALU.arith_shift_right))
            step(v.tensor_copy(gfirst[:, :], tot_i[:, :]))
            for q in range(2):
                bins = slice(q * NT, (q + 1) * NT)
                last = v.tensor_tensor_scan(gend[:, bins], ones_e[:, 0:NT], gfirst[:, bins], 0.0, ALU.mult, ALU.add)
            step(last)
            step(v.tensor_tensor(gfirst[:, :], gend[:, :], gfirst[:, :], ALU.subtract))
            step(v.scalar_tensor_tensor(base[:, :], gfirst[:, :], float(P), bank[7][:, 0:2 * NT], ALU.mult, ALU.add))
            v.tensor_scalar(base[:, :], base[:, :], -1.0, None, ALU.add).then_inc(s_first, 1)
            dve.wait_ge(s_first, 1)
            for q in range(2):
                c = slice(PCOL[q], PEND[q])
                for b in range(NT):
                    n = q * NT + b
                    last = v.scalar_tensor_tensor(scan_v[:, b, c], scan_v[:, b, c], base[:, n:n + 1], inbin_v[:, b, c], ALU.add, ALU.mult)
            step(last)
            step(v.tensor_reduce(pos_f[:, :], scan_v.rearrange("p b c -> p c b"), AX.X, ALU.add))
            step(v.tensor_copy(tmp_i[:, :], pos_f[:, :]))
            step(v.tensor_scalar(tmp2_i[:, :], tmp_i[:, :], SH, None, ALU.arith_shift_right))
            step(v.tensor_scalar(tmp_i[:, :], tmp_i[:, :], P - 1, None, ALU.bitwise_and))
            v.tensor_copy(group_f[:, :], tmp2_i[:, :])
            step(v.tensor_copy(slot16[:, :], tmp_i[:, :]))
            step(v.tensor_scalar(tmp_i[:, :], src_i[:, :], P - 1, None, ALU.bitwise_and))
            v.tensor_copy(val16[0][:, :], tmp_i[:, :])
            v.tensor_scalar(val16[1][:, :], dst_i[:, :], float(-DOFF), None, ALU.add)
            step(v.tensor_copy(val16[2][:, :], ew[:, :]))
            step(v.tensor_tensor(pos_f[:, :], ew[:, :], val16[2][:, :], ALU.subtract))
            step(v.tensor_copy(val16[3][:, :], pos_f[:, :]))
            step(v.tensor_tensor(val16[4][:, :], pos_f[:, :], val16[3][:, :], ALU.subtract))

            dve.wait_ge(s_firstT, 1)
            step(v.tensor_copy(first_cols[0:NT, :], bank[7][0:NT, 128:130]))
            for q in range(2):
                last = v.tensor_scalar(reached[0:NT, PG[q]:PG[q] + NGP[q]], groups16[0:NT, 0:NGP[q]], first_cols[0:NT, q:q + 1], None, ALU.is_ge)
            last.then_inc(s_reached, 1)
            dve.wait_ge(s_binrow, 1)
            v.tensor_scalar(bin_i[:, :], bank[6][:, 0:NG], -1.0, None, ALU.add)
            v.memset(scan[:, 0:NT * D], 0.0).then_inc(s_acc, PR)

            def onehots(q, k, n, r):
                c = k * UE + PCOL[q]

                def over_slots(ap):
                    return ap[:, bass.ds(c, UE)].rearrange("p (s u) -> p s u", s=1).broadcast_to([P, P, UE])

                def value(f):
                    o = put_v[:, r, f, :, :]
                    return v.tensor_tensor(o.bitcast(f16) if f < 2 else o, at_slot[:, r, :, :], over_slots(val16[f]), ALU.mult)

                for u in range(UE):
                    if u == 0:
                        dve.wait_ge(s_onehot_free, n * UE + UE)
                        v.tensor_tensor(at_slot[:, r, :, :], slots16[:, :, :], over_slots(slot16), ALU.is_equal).then_inc(s_at, 1)
                    last = v.tensor_scalar(in_group[:, r, u, 0:NGP[q]], groups16[:, 0:NGP[q]], group_f[:, bass.ds(c + u, 1)], None, ALU.is_equal)
                    if u == 1:
                        dve.wait_ge(s_at, n + 1)
                    if u % 2:
                        last = value(u // 2)
                    if u == UE - 1:
                        last = value(4)
                        last.then_inc(s_onehot, 1)
                    yield

            def batch(*which):
                for _ in onehots(*which):
                    pass

            def lists(q):
                dve.wait_ge(s_sorted, q + 1)
                g = slice(PG[q], PG[q] + NGP[q])
                v.tensor_scalar(node_i[:, g], bank[1][:, 0:NGP[q]], float(DOFF), None, ALU.add).then_inc(s_lists, 1)
                if q == 0:
                    v.memset(slot_src[:, NG:], 0.0)
                    v.memset(slot_ew[:, NG:], 0.0)
                v.tensor_copy(slot_src[:, g], bank[0][:, 0:NGP[q]]).then_inc(s_lists, 1)
                v.tensor_copy(slot_ew[:, g], bank[2][:, 0:NGP[q]]).then_inc(s_lists, 1)
                dve.wait_ge(s_lists, 3 * q + 3)

            def matrix(g, j):
                dve.wait_ge(s_part, g + (RING - TURN + 1))
                v.tensor_scalar(mat[:, j, :], slots32[:, :], slot_src[:, bass.ds(g, 1)], slot_ew[:, bass.ds(g, 1)],
                                ALU.is_equal, ALU.mult).then_inc(s_mat, 1)

            def accumulate(g, j, tile):
                dve.wait_ge(s_part, g + (RING + 1))
                dve.wait_ge(s_acc, g + PR)
                v.tensor_tensor(side[:, tile, :], side[:, tile, :], bank[3 + j % PR][:, 0:D], ALU.add).then_inc(s_acc, 1)

            def turn(n, beside=None):
                _, tiles = nc.values_load_multi_w_load_instructions(
                    bin_i[0:1, bass.ds(n * TURN, TURN)], engines=[DVE], min_val=0, max_val=NT - 1)
                for j in range(TURN):
                    matrix(n * TURN + (j + AHEAD), (j + AHEAD) % TURN)
                    if beside is not None:
                        next(beside)
                    accumulate(n * TURN + j, j, bass.ds(tiles[j], 1))

            with dve.Fori(0, BATCHES[0] // 2) as i:
                for r in range(2):
                    batch(0, i * 2 + r, i * 2 + r, r)
            batch(0, BATCHES[0] - 1, BATCHES[0] - 1, 0)
            batch(1, 0, BATCHES[0], 1)
            lists(0)
            for j in range(AHEAD):
                matrix(j, j)
            with dve.Fori(0, BATCHES[1] // 2 - 1) as i:
                for r in range(2):
                    turn(i * 2 + r, onehots(1, i * 2 + (r + 1), i * 2 + (BATCHES[0] + r + 1), r))
            turn(BATCHES[1] - 2, onehots(1, BATCHES[1] - 1, BATCHES[0] + BATCHES[1] - 1, 0))
            turn(BATCHES[1] - 1)
            lists(1)
            with dve.Fori(BATCHES[1] // 2, NG // RING) as i:
                for r in range(2):
                    turn(i * 2 + r)
            turn(NG // TURN - 1)

            dve.wait_ge(s_wload, WLOADS * 16)
            step(v.tensor_copy(gb16, gb[0:BROWS, :]))
            step(v.tensor_tensor(gb[0:BROWS, :], gb[0:BROWS, :], gb16, ALU.subtract))
            v.tensor_copy(gb16[32:64, :], gb[32:64, :])
            step(v.tensor_copy(gb16[64:BROWS, :], gb[64:BROWS, :]))
            v.tensor_tensor(gb16[64:BROWS, :], gb[64:BROWS, :], gb16[64:BROWS, :], ALU.subtract).then_inc(s_gb, 1)

            dve.sem_inc(s_lk, 2)
            dve.sem_inc(s_x1, 6)

            def x1_tile(t, r):
                dve.wait_ge(s_slope, t + 1)
                both = lk[:, r, :, :].rearrange("p k d -> p (k d)")
                v.tensor_tensor(both, both, bank[(2, 7)[r]][:, :], ALU.max).then_inc(s_lk, 1)
                dve.wait_ge(s_lk, t + 3)
                v.tensor_tensor(xs[:, t, :], xs[:, t, :], lk[:, r, 0, :], ALU.add).then_inc(s_x1, 1)
                dve.wait_ge(s_x1, t * 3 + 7)
                v.tensor_tensor(xs[:, t, :], xs[:, t, :], lk[:, r, 1, :], ALU.add).then_inc(s_x1, 1)
                dve.wait_ge(s_x1, t * 3 + 8)
                v.bn_stats(stats[:, t, :], xs[:, t, :]).then_inc(s_x1, 1)

            with dve.Fori(0, NT // 2) as i:
                for r in range(2):
                    x1_tile(i * 2 + r, r)
            x1_tile(NT - 1, 0)
            dve.wait_ge(s_x1, 3 * NT + 6)
            aggregate()
            rstd(2)

            v.memset(y_last[:, :, :], 0.0).then_inc(s_ylast, 1)
            step(v.memset(pgroup_f[:, K * NT:], -1.0))
            step(v.memset(pslot16[:, K * NT:], 0.0))
            step(v.memset(ptok16[:, K * NT:], 0.0))
            step(v.memset(pk16[:, K * NT:], 0.0))
            for k in range(K):
                v.memset(pk16[:, k * NT:(k + 1) * NT], float(k + 1))
                last = v.tensor_copy(ptok16[:, k * NT:(k + 1) * NT], tokens[:, :])
            step(last)

            dve.wait_ge(s_logit, NT + 2)

            def over_tiles(col):
                return col.rearrange("p (x t) -> p x t", t=1).broadcast_to([P, X, NT])

            def over_experts(row):
                return row.rearrange("p (x t) -> p x t", x=1).broadcast_to([P, X, NT])

            step(v.tensor_tensor(logits, bank[5][:, 0:NT * X].rearrange("p (t x) -> p x t", x=X), over_tiles(gateb[:, :]), ALU.add))
            for k in range(K):
                step(v.tensor_reduce(top[k][:, :], logits.rearrange("p x t -> p t x"), AX.X, ALU.max))
                step(v.tensor_tensor(is_top, logits, over_experts(top[k][:, :]), ALU.is_equal))
                step(v.tensor_tensor(is_top, is_top, experts[:, :, :], ALU.mult))
                step(v.tensor_reduce(pick[:, :], is_top.rearrange("p x t -> p t x"), AX.X, ALU.min))
                step(v.tensor_tensor(chosen[k], experts[:, :, :], over_experts(pick[:, :]), ALU.is_equal))
                if k == 0:
                    step(v.scalar_tensor_tensor(logits, chosen[k], -BIG, logits, ALU.mult, ALU.add))
                step(v.tensor_scalar(chosen[k][:, :, NT - 1], chosen[k][:, :, NT - 1], valid[:, :], None, ALU.mult))
            v.tensor_tensor(gain[1][:, :], top[1][:, :], top[0][:, :], ALU.subtract).then_inc(s_gap, 1)
            step(v.tensor_tensor(spread, chosen[0], chosen[1], ALU.add))
            for e in range(X):
                last = v.tensor_tensor_scan(rank[:, e, :], ones_e[:, 0:NT], spread[:, e, :], 0.0, ALU.mult, ALU.add)
            step(last)
            v.tensor_copy(bases[:, :], rank[:, :, NT - 1]).then_inc(s_bcnt, 1)
            dve.wait_ge(s_exp, 1)
            step(v.tensor_scalar(gain[0][:, :], gain[1][:, :], 1.0, None, ALU.add))
            step(v.reciprocal(gain[0][:, :], gain[0][:, :]))
            step(v.tensor_tensor(gain[1][:, :], gain[1][:, :], gain[0][:, :], ALU.mult))
            dve.wait_ge(s_boff, 1)
            step(v.tensor_scalar(btot_i[:, :], bank[6][:, 64:64 + X], float(BS - 1), None, ALU.add))
            step(v.tensor_scalar(btot_i[:, :], btot_i[:, :], BS.bit_length() - 1, None, ALU.arith_shift_right))
            step(v.tensor_copy(bfirst[:, :], btot_i[:, :]))
            step(v.tensor_tensor_scan(bend[:, :], ones_e[:, 0:X], bfirst[:, :], 0.0, ALU.mult, ALU.add))
            v.tensor_tensor(bfirst[:, :], bend[:, :], bfirst[:, :], ALU.subtract).then_inc(s_bfirst, 1)
            dve.wait_ge(s_bfirst, 1)
            step(v.scalar_tensor_tensor(bases[:, :], bfirst[:, :], float(BS), bank[6][:, 0:X], ALU.mult, ALU.add))
            step(v.tensor_tensor(rank, rank, over_tiles(bases[:, :]), ALU.add))
            for k in range(K):
                step(v.tensor_tensor(spread, rank, chosen[k], ALU.mult))
                step(v.tensor_reduce(place_f[:, k * NT:(k + 1) * NT], spread.rearrange("p x t -> p t x"), AX.X, ALU.add))
            step(v.tensor_scalar(place_i[:, 0:K * NT], place_f[:, 0:K * NT], -1.0, None, ALU.add))
            step(v.tensor_scalar(place2_i[:, 0:K * NT], place_i[:, 0:K * NT], SH, None, ALU.arith_shift_right))
            step(v.tensor_scalar(place_i[:, 0:K * NT], place_i[:, 0:K * NT], P - 1, None, ALU.bitwise_and))
            step(v.tensor_copy(pgroup_f[:, 0:K * NT], place2_i[:, 0:K * NT]))
            step(v.tensor_copy(pslot16[:, 0:K * NT], place_i[:, 0:K * NT]))
            dve.wait_ge(s_bfirstT, 1)
            step(v.tensor_copy(first_col[0:X, :], bank[7][0:X, 128:129]))
            v.tensor_scalar(breached[0:X, :], groups16[0:X, 0:NB], first_col[0:X, :], None, ALU.is_ge).then_inc(s_breached, 1)
            dve.wait_ge(s_brow, 1)
            v.tensor_scalar(expert_i[:, :], bank[7][:, 0:NB], -1.0, None, ALU.add)
            step(v.tensor_scalar(pair_i[:, :], bend[:, X - 1:X], -1.0, None, ALU.add))
            v.tensor_scalar(pair_i[:, :], pair_i[:, :], 1, None, ALU.arith_shift_right).then_inc(s_blocks, 1)

            for n in range(NA // UE):
                r = n % 2
                if n >= 2:
                    dve.wait_ge(s_pfree, n - 1)
                c = slice(n * UE, (n + 1) * UE)

                def spread_over(ap):
                    return ap[:, c].rearrange("p (s u) -> p s u", s=1).broadcast_to([P, P, UE])
                v.tensor_tensor(at_slot[:, r, :, :], slots16[:, :, :], spread_over(pslot16), ALU.is_equal).then_inc(s_pat, 1)
                v.tensor_tensor(in_group[:, r, :, 0:NS], groups16[:, 0:NS].rearrange("p (u g) -> p u g", u=1).broadcast_to([P, UE, NS]),
                                pgroup_f[:, c].rearrange("p (u g) -> p u g", g=1).broadcast_to([P, UE, NS]), ALU.is_equal)
                dve.wait_ge(s_pat, n + 1)
                v.tensor_tensor(put_v[:, r, 0, :, :].bitcast(f16), at_slot[:, r, :, :], spread_over(ptok16), ALU.mult)
                v.tensor_tensor(put_v[:, r, 1, :, :].bitcast(f16), at_slot[:, r, :, :], spread_over(pk16), ALU.mult).then_inc(s_pone, 1)
            dve.wait_ge(s_placed, 1)
            step(v.tensor_scalar(empty_f[:, :], bank[1][:, 0:NS], 0.0, float(NOROW), ALU.is_equal, ALU.mult))
            step(v.tensor_tensor(empty_f[:, :], empty_f[:, :], bank[1][:, 0:NS], ALU.add))
            step(v.scalar_tensor_tensor(row_f[:, :], bank[0][:, 0:NS], float(K), empty_f[:, :], ALU.mult, ALU.add))
            v.tensor_scalar(row_i[:, :], row_f[:, :], float(K * DOFF - 1), None, ALU.add).then_inc(s_routes, 1)
            v.tensor_scalar(token_i[:, :], bank[0][:, 0:NS], float(DOFF), None, ALU.add).then_inc(s_routes, 1)

            dve.wait_ge(s_routes, 2)
            dve.sem_inc(s_ysb, 4)

            v.tensor_tensor(xs[:, :, :], xs[:, :, :], bet[:, :].rearrange("p (t d) -> p t d", t=1).broadcast_to([P, NT, D]), ALU.add)

            def results(b, i, r):
                dve.wait_ge(s_y, b + 3)
                dve.wait_ge(s_bias[r], i * 16 + 16)
                for q in range(2):
                    v.tensor_tensor(y_sb[:, r, q, :], bank[YB[r][q]][:, 0:D], b2_sb[:, r, :], ALU.add).then_inc(s_ysb, 1)

            dve.wait_ge(s_blocks, 1)
            end = last_pair(DVE)
            for r in range(2):
                results(r, 0, r)
            with dve.Fori(1, end + 1) as i:
                for r in range(2):
                    dve.wait_ge(s_yout[r], i * 32)
                    results(i * 2 + r, i, r)

            def ffn_sum(t, y, k0):
                tile = hs[:, bass.ds(t, 1), :].rearrange("p t d -> p (t d)")
                c = bass.ds(t, 1)
                v.scalar_tensor_tensor(tile, y[:, 0, :], gain[0][:, c], tile, ALU.mult, ALU.add).then_inc(s_sum, 1)
                dve.wait_ge(s_sum, k0 + 1)
                v.scalar_tensor_tensor(tile, y[:, 1, :], gain[1][:, c], tile, ALU.mult, ALU.add).then_inc(s_sum, 1)
                dve.wait_ge(s_sum, k0 + 2)
                v.bn_stats(stats[:, bass.ds(t, 1), :].rearrange("p t s -> p (t s)"), tile).then_inc(s_sum, 1)

            dve.sem_inc(s_sum, YR * 3)
            with dve.Fori(0, (NT - 1) // YR) as i:
                for j in range(YR):
                    dve.wait_ge(s_yin[j], i * 16 + 16)
                    ffn_sum(i * YR + j, y_in[:, j, :, :], (i * YR + (j + YR)) * 3)
            dve.wait_ge(s_ylast, 17)
            ffn_sum(NT - 1, y_last, (NT - 1 + YR) * 3)
            dve.wait_ge(s_sum, (NT + YR) * 3)
            aggregate()
            rstd(3)
            with dve.Fori(0, NT) as t:
                tile = hs[:, bass.ds(t, 1), :].rearrange("p t d -> p (t d)")
                dve.wait_ge(s_norm, t + 1)
                v.tensor_tensor(tile, tile, gam[:, :], ALU.mult).then_inc(s_fin, 1)
                dve.wait_ge(s_fin, t * 2 + 1)
                v.tensor_tensor(tile, tile, xs[:, bass.ds(t, 1), :].rearrange("p t d -> p (t d)"), ALU.add).then_inc(s_fin, 1)

        @block.scalar
        def _(act):
            a = nc.scalar
            act.wait_ge(s_const, 12)
            act.wait_ge(s_var, 1)

            def std(n):
                act.wait_ge(s_var, n)
                a.activation(ln[2][:, :], mv[:, :, 1], ACT.Sqrt, bias=eps_col[:, :]).then_inc(s_std, 1)
                act.wait_ge(s_rstd, n)

            def normalise(tiles, t, done):
                c = bass.ds(t, 1)
                a.activation(hs[:, c, :].rearrange("p t d -> p (t d)"), tiles[:, c, :].rearrange("p t d -> p (t d)"), ACT.Identity,
                             bias=ln[3][:, c], scale=ln[1][:, c]).then_inc(done, 1)

            std(1)
            with act.Fori(0, NT) as t:
                normalise(xs, t, s_h)

            def copy_T(t, r):
                act.wait_ge(s_uvT, t + 3)
                act.wait_ge(s_o, t + 1)
                a.activation(uvT[:, r, :, :].rearrange("p c n -> p (c n)"), bank[r][:, :], ACT.Copy).then_inc(s_uvTc, 1)

            def slope(t, r):
                act.wait_ge(s_o, t + 3)
                act.wait_ge(s_x1, t * 3 + 3)
                a.activation(lk[:, r, :, :].rearrange("p k d -> p (k d)"), bank[(2, 7)[r]][:, :], ACT.Copy, scale=SLOPE).then_inc(s_slope, 1)

            act.sem_inc(s_uvTc, 2)
            act.wait_ge(s_acc, NG + PR)
            copy_T(0, 0)
            with act.Fori(0, NT // 2) as i:
                for r in range(2):
                    copy_T(i * 2 + (r + 1), 1 - r)
                    slope(i * 2 + r, r)
            slope(NT - 1, 0)

            def copy_zT(t, r):
                act.wait_ge(s_zTg, t + 1)
                act.wait_ge(s_logit, t + 1)
                a.activation(zTg[:, r, :, :].rearrange("p c n -> p (c n)"), bank[3 + r][:, 0:D], ACT.Copy).then_inc(s_zTgc, 1)

            act.sem_inc(s_zTgc, 2)
            std(2)
            normalise(xs, 0, s_z)
            with act.Fori(0, NT // 2) as i:
                for r in range(2):
                    normalise(xs, i * 2 + (r + 1), s_z)
                    copy_zT(i * 2 + r, r)
            copy_zT(NT - 1, 0)

            act.wait_ge(s_gap, 1)
            a.activation(gain[1][:, :], gain[1][:, :], ACT.Exp).then_inc(s_exp, 1)
            act.wait_ge(s_b1T, 1)
            a.activation(b1T[:, :], bank[4][:, 0:X * KF], ACT.Copy).then_inc(s_b1, 1)
            act.wait_ge(s_b1, 1)

            def copy_block(b, r):
                act.wait_ge(s_zgT, b + 3)
                act.wait_ge(s_hid, b * 2 + 2)
                a.activation(zT[:, r, :, :].rearrange("p c n -> p (c n)"), bank[1 + r][:, :], ACT.Copy).then_inc(s_zTc, 1)

            def relus(b, r, e):
                act.wait_ge(s_y, b + 1)
                for c in range(KF):
                    act.wait_ge(s_hid, b * 2 + (5 + c // 2))
                    a.activation(hT[:, r, c, :], bank[3 + c // 2][:, (c % 2) * BS:(c % 2 + 1) * BS], ACT.Relu,
                                 bias=b1T[:, bass.ds(e * KF + c, 1)]).then_inc(s_relu, 1)

            def block_experts(b):
                _, es = nc.values_load_multi_w_load_instructions(expert_i[0:1, bass.ds(b, 2)], engines=[ACTE], min_val=0, max_val=X - 1)
                return es

            act.wait_ge(s_blocks, 1)
            act.sem_inc(s_zTc, 2)
            act.sem_inc(s_relu, 4)
            copy_block(0, 0)
            end = last_pair(ACTE)
            with act.Fori(0, end) as i:
                es = block_experts(i * 2)
                for r in range(2):
                    copy_block(i * 2 + (r + 1), 1 - r)
                    relus(i * 2 + r, r, es[r])
            es = block_experts(end * 2)
            copy_block(end * 2 + 1, 1)
            for r in range(2):
                relus(end * 2 + r, r, es[r])

            std(3)
            with act.Fori(0, NT) as t:
                normalise(hs, t, s_norm)

        @block.tensor
        def _(pe):
            t_ = nc.tensor
            pe.wait_ge(s_const, 12)
            pe.wait_ge(s_cnt, 1)
            t_.matmul(bank[7][:, 0:2 * NT], below[:, :], cnt[:, :], start=True, stop=True)
            t_.matmul(bank[7][:, 64:64 + 2 * NT], ones[:, :], cnt[:, :], start=True, stop=True).then_inc(s_off, 1)
            pe.wait_ge(s_first, 1)
            for q in range(2):
                last = t_.matmul(bank[7][0:NT, 128 + q:129 + q], gfirst[0:1, q * NT:(q + 1) * NT], ones[0:1, 0:1], start=True, stop=True)
            last.then_inc(s_firstT, 1)
            pe.wait_ge(s_reached, 1)
            t_.matmul(bank[6][:, 0:NG], ones_e[0:NT, 0:P], reached[0:NT, :], start=True, stop=True).then_inc(s_binrow, 1)

            def sort_edge(q, first):
                for f in range(3):
                    last = t_.matmul(bank[f][:, 0:NGP[q]], zeros16[:, 0:P], zeros16[:, 0:NGP[q]], start=first, stop=not first)
                return last

            def sort(q, n, r, u):
                if u == 0:
                    pe.wait_ge(s_onehot, n + 1)
                for f in range(5):
                    o = put_v[:, r, f, :, u]
                    last = t_.matmul(bank[min(f, 2)][:, 0:NGP[q]], o.bitcast(f16) if f < 2 else o, in_group[:, r, u, 0:NGP[q]],
                                     start=False, stop=False)
                if u == UE - 1:
                    last.then_inc(s_onehot_free, UE)

            def group(n, i, r, j):
                g = n * TURN + j
                pe.wait_ge(s_mat, g + 1)
                pe.wait_ge(s_acc, g + 1)
                pe.wait_ge(s_got[r * TURN + j], i * 16 + 16)
                t_.matmul(bank[3 + j % PR][:, 0:D], mat[:, j, :], ring[:, r * TURN + j, :], start=True, stop=True).then_inc(s_part, 1)

            sort_edge(0, True).then_inc(s_onehot_free, 2 * UE)
            with pe.Fori(0, BATCHES[0] // 2) as i:
                for r in range(2):
                    for u in range(UE):
                        sort(0, i * 2 + r, r, u)
            for u in range(UE):
                sort(0, BATCHES[0] - 1, 0, u)
            sort_edge(0, False).then_inc(s_sorted, 1)
            pe.sem_inc(s_part, RING)
            pe.wait_ge(s_lists, 3)
            sort_edge(1, True)
            with pe.Fori(0, BATCHES[1] // 2) as i:
                for r in range(2):
                    for j in range(TURN):
                        group(i * 2 + r, i, r, j)
                        sort(1, i * 2 + (BATCHES[0] + r), 1 - r, j)
            sort_edge(1, False).then_inc(s_sorted, 1)
            with pe.Fori(BATCHES[1] // 2, NG // RING) as i:
                for r in range(2):
                    for j in range(TURN):
                        group(i * 2 + r, i, r, j)
            for j in range(TURN):
                group(NG // TURN - 1, NG // RING, 0, j)

            def transposes(t, r):
                pe.wait_ge(s_uv, t + 1)
                pe.wait_ge(s_uvTc, t + 1)
                for k in range(2):
                    for c in range(KD):
                        q = k * KD + c
                        last = t_.transpose(bank[r][:, q * P:(q + 1) * P], uv[:, r, k, c * P:(c + 1) * P], ident[:, :])
                last.then_inc(s_uvT, 1)

            def products(t, r):
                pe.wait_ge(s_uvTc, t + 3)
                pe.wait_ge(s_lk, t + 1)
                o = bank[(2, 7)[r]]
                for k in range(2):
                    t_.matmul(o[:, k * D:(k + 1) * D], ones_e[0:BROWS, 0:P], gb16[:, k * D:(k + 1) * D], start=True, stop=False)
                    for c in range(KD):
                        last = t_.matmul(o[:, k * D:(k + 1) * D], uvT[:, r, k * KD + c, :], gw[:, k, c, :], start=False, stop=c == KD - 1)
                last.then_inc(s_o, 1)

            pe.wait_ge(s_wload, WLOADS * 16)
            pe.wait_ge(s_gb, 1)
            pe.sem_inc(s_uvT, 2)
            pe.sem_inc(s_o, 2)
            transposes(0, 0)
            with pe.Fori(0, NT // 2) as i:
                for r in range(2):
                    transposes(i * 2 + (r + 1), 1 - r)
                    products(i * 2 + r, r)
            products(NT - 1, 0)

            def gate_transposes(t, r):
                pe.wait_ge(s_z, t + 1)
                pe.wait_ge(s_zTgc, t + 1)
                for c in range(KD):
                    last = t_.transpose(bank[3 + r][:, c * P:(c + 1) * P], hs[:, bass.ds(t, 1), c * P:(c + 1) * P].rearrange("p t d -> p (t d)"), ident[:, :])
                last.then_inc(s_zTg, 1)

            def gate_products(t, r):
                pe.wait_ge(s_zTgc, t + 3)
                for c in range(KD):
                    last = t_.matmul(bank[5][:, bass.ds(t * X, X)], zTg[:, r, c, :], gatew[:, c, :], start=c == 0, stop=c == KD - 1)
                last.then_inc(s_logit, 1)

            pe.sem_inc(s_logit, 2)
            gate_transposes(0, 0)
            for t in range(NT):
                if t + 1 < NT:
                    gate_transposes(t + 1, 1 - t % 2)
                gate_products(t, t % 2)

            pe.wait_ge(s_bcnt, 1)
            t_.matmul(bank[6][:, 0:X], below[:, :], bases[:, :], start=True, stop=True)
            t_.matmul(bank[6][:, 64:64 + X], ones[:, :], bases[:, :], start=True, stop=True).then_inc(s_boff, 1)
            t_.transpose(bank[4][:, 0:X * KF], b1_rows[:, :], ident[0:X * KF, 0:X * KF]).then_inc(s_b1T, 1)
            pe.wait_ge(s_bfirst, 1)
            t_.matmul(bank[7][0:X, 128:129], bfirst[0:1, :], ones[0:1, 0:1], start=True, stop=True).then_inc(s_bfirstT, 1)
            pe.wait_ge(s_breached, 1)
            t_.matmul(bank[7][:, 0:NB], ones_e[0:X, 0:P], breached[0:X, :], start=True, stop=True).then_inc(s_brow, 1)

            for n in range(NA // UE):
                pe.wait_ge(s_pone, n + 1)
                for u in range(UE):
                    for f in range(2):
                        last = t_.matmul(bank[f][:, 0:NS], put_v[:, n % 2, f, :, u].bitcast(f16), in_group[:, n % 2, u, 0:NS],
                                         start=n == 0 and u == 0, stop=n == NA // UE - 1 and u == UE - 1)
                last.then_inc(s_pfree, 1)
            pe.wait_ge(s_pfree, NA // UE)
            pe.sem_inc(s_placed, 1)

            def block_transposes(b, i, r):
                for q in range(2):
                    pe.wait_ge(s_zg[r * 2 + q], i * 16 + 16)
                pe.wait_ge(s_zTc, b + 1)
                for c in range(KD):
                    for q in range(2):
                        last = t_.transpose(bank[1 + r][:, c * BS + q * P:c * BS + (q + 1) * P], zg[:, r, q, c * P:(c + 1) * P], ident[:, :])
                last.then_inc(s_zgT, 1)

            def block(b, i, r):
                pe.wait_ge(s_w[r], i * 32 + 32)
                pe.wait_ge(s_zTc, b + 3)
                for c in range(KF):
                    pe.wait_ge(s_relu, b * 4 + (c // 2 * 2 + 2))
                    for k in range(KD):
                        last = t_.matmul(bank[3 + c // 2][:, (c % 2) * BS:(c % 2 + 1) * BS], w1_sb[:, r, k, c * P:(c + 1) * P], zT[:, r, k, :],
                                         start=k == 0, stop=k == KD - 1)
                    if c % 2:
                        last.then_inc(s_hid, 1)
                pe.wait_ge(s_ysb, b * 2 + 2)
                for c in range(KF):
                    pe.wait_ge(s_relu, b * 4 + (c + 5))
                    for q in range(2):
                        last = t_.matmul(bank[YB[r][q]][:, 0:D], hT[:, r, c, q * P:(q + 1) * P], w2_sb[:, r, c, :], start=c == 0, stop=c == KF - 1)
                last.then_inc(s_y, 1)

            pe.wait_ge(s_b1, 1)
            pe.sem_inc(s_zgT, 2)
            pe.sem_inc(s_hid, 4)
            pe.sem_inc(s_y, 2)
            block_transposes(0, 0, 0)
            pe.wait_ge(s_blocks, 1)
            end = last_pair(mybir.EngineType.PE)
            with pe.Fori(0, end) as i:
                for r in range(2):
                    block_transposes(i * 2 + (r + 1), i + r, 1 - r)
                    block(i * 2 + r, i, r)
            block_transposes(end * 2 + 1, end, 1)
            for r in range(2):
                block(end * 2 + r, end, r)


_INS = ['x', 'src', 'dst', 'edge_weight', 'L0_gnn_W1', 'L0_gnn_b1', 'L0_gnn_W2', 'L0_gnn_b2', 'L0_ffn_gate_w',
        'L0_ffn_gate_b', 'L0_ffn_w1', 'L0_ffn_b1', 'L0_ffn_w2', 'L0_ffn_b2', 'L0_ffn_gamma', 'L0_ffn_beta']


def kernel(**inputs):
    import numpy as np
    import concourse.bacc as bacc
    from concourse.bass_utils import run_bass_kernel_spmd as run

    nc = bacc.Bacc("TRN2", target_bir_lowering=False, num_devices=1)
    arrays, args = {}, []
    for name in _INS:
        a = np.ascontiguousarray(inputs[name])
        arrays[f"in_{name}"] = a
        args.append(nc.dram_tensor(f"in_{name}", a.shape, mybir.dt.from_np(a.dtype), kind="ExternalInput").ap())
    args.append(nc.dram_tensor("out_x", (N, D), f32, kind="ExternalOutput").ap())
    build(nc, *args)
    return run(nc, [arrays], core_ids=[0]).results[0]["out_x"]
```
